# Optimizing a Trainium2 kernel written in Bass

```python
import numpy as np
import jax
import jax.numpy as jnp

def _softmax(x, axis=-1):
    return jax.nn.softmax(x, axis=axis)

def _gelu(x):
    return jax.nn.gelu(x, approximate=True)

def _silu(x):
    return jax.nn.silu(x)

def _sigmoid(x):
    return jax.nn.sigmoid(x)

def _layernorm(x, axis=-1, eps=1e-05):
    m = jnp.mean(x, axis=axis, keepdims=True)
    v = jnp.var(x, axis=axis, keepdims=True)
    return (x - m) / jnp.sqrt(v + eps)

def _scatter_add(tgt, idx, src, axis=0):
    return tgt.at[idx].add(src)

def _segment_sum(src, seg, n):
    return jax.ops.segment_sum(src, seg, n)
kernel_name = 'mk_conv_preact_d2_conv_nchw128_r4_6f4025'

def setup_inputs(seed: int=0):
    np.random.seed(seed)
    _w = jnp.asarray

    def _rec_inputs():
        import jax
        import jax.numpy as jnp
        _gk = jax.random.key(seed)
        x = -7.109e-05 + 0.9999 * jax.random.normal(jax.random.fold_in(_gk, 1), (8, 32, 64, 64), jnp.float32)
        return x
    x = _rec_inputs()

    def _L0_conv_setup():
        import jax, jax.numpy as jnp
        import numpy as np
        B, CIN, COUT, NH, M1, M2, H, W = (8, 32, 32, 1, 32, 32, 64, 64)
        HC = COUT // NH
        key = jax.random.key(seed)
        k1, k2, k3 = jax.random.split(key, 3)
        x = jax.random.normal(k1, (B, CIN, H, W), jnp.float32)
        scales = jnp.asarray(0.01 * 2.0 ** np.arange(NH), jnp.float32)
        weight = jax.random.normal(k2, (NH, HC, HC, M1, M2), jnp.float32) * scales[:, None, None, None, None]
        fc_w = jax.random.normal(k3, (COUT, CIN), jnp.float32) * np.float32(np.sqrt(2.0 / (CIN + COUT)))
        fc_b = jnp.zeros((COUT,), jnp.float32)
        return {'x': x, 'weight': weight, 'fc_w': fc_w, 'fc_b': fc_b}
    _L0_conv_all = _L0_conv_setup()
    _L0_conv_in = {k: v for k, v in _L0_conv_all.items() if k in ('weight', 'fc_w', 'fc_b')}
    del _L0_conv_all

    def _L1_conv_setup():
        import jax, jax.numpy as jnp
        from jax import lax
        import numpy as np
        B, CIN, COUT, H, W = (16, 32, 32, 32, 32)
        K_NUM, KH, KW = (16, 3, 3)
        key = jax.random.key(seed)
        k1, k2, k3 = jax.random.split(key, 3)
        x = jax.random.normal(k1, (B, CIN, H, W), dtype=jnp.float32)
        dft_weight = jax.random.normal(k2, (K_NUM, COUT, CIN, KH, KW, 2), dtype=jnp.float32) * 0.1
        ksm_w = jax.random.normal(k3, (K_NUM, CIN), dtype=jnp.float32) * 0.05
        bias = jnp.zeros((COUT,), dtype=jnp.float32)
        fbm_scale = jnp.ones((1, COUT, 1, 1), dtype=jnp.float32)
        return {'x': x, 'dft_weight': dft_weight, 'ksm_w': ksm_w, 'bias': bias, 'fbm_scale': fbm_scale}
    _L1_conv_all = _L1_conv_setup()
    _L1_conv_in = {k: v for k, v in _L1_conv_all.items() if k in ('dft_weight', 'ksm_w', 'bias', 'fbm_scale')}
    del _L1_conv_all
    return {'x': x, 'L0_conv_weight': _L0_conv_in['weight'], 'L0_conv_fc_w': _L0_conv_in['fc_w'], 'L0_conv_fc_b': _L0_conv_in['fc_b'], 'L1_conv_dft_weight': _L1_conv_in['dft_weight'], 'L1_conv_ksm_w': _L1_conv_in['ksm_w'], 'L1_conv_bias': _L1_conv_in['bias'], 'L1_conv_fbm_scale': _L1_conv_in['fbm_scale']}

def reference(x, L0_conv_weight, L0_conv_fc_w, L0_conv_fc_b, L1_conv_dft_weight, L1_conv_ksm_w, L1_conv_bias, L1_conv_fbm_scale):
    import jax
    import jax.numpy as jnp

    def _L0_conv_ref(x, weight, fc_w, fc_b):
        import jax, jax.numpy as jnp
        import numpy as np
        B, CIN, COUT, NH, M1, M2, H, W = (8, 32, 32, 1, 32, 32, 64, 64)
        HC = COUT // NH
        x_ft = jnp.fft.rfftn(x, axes=(-2, -1))
        Wf = x_ft.shape[-1]
        m1, m2 = (min(M1, H), min(M2, Wf))
        w_c = weight[..., :m1, :m2].astype(x_ft.dtype)
        blk = jnp.einsum('bimn,hiomn->bhomn', x_ft[:, :, :m1, :m2], w_c)
        blk = blk.reshape(x.shape[0], NH * HC, m1, m2)
        out_ft = jnp.zeros((x.shape[0], COUT, H, Wf), x_ft.dtype).at[:, :, :m1, :m2].set(blk)
        xr = jnp.fft.irfftn(out_ft, s=(H, W), axes=(-2, -1))
        return jnp.einsum('bchw,oc->bohw', xr, fc_w) + fc_b[None, :, None, None]

    def _L1_conv_ref(x, dft_weight, ksm_w, bias, fbm_scale):
        import jax, jax.numpy as jnp
        from jax import lax
        import numpy as np
        B, CIN, COUT, H, W = (16, 32, 32, 32, 32)
        K_NUM, KH, KW = (16, 3, 3)
        b, cin, h, w = x.shape
        k_num, cout = (dft_weight.shape[0], dft_weight.shape[1])
        pooled = x.mean(axis=(2, 3))
        att = jax.nn.sigmoid(pooled @ ksm_w.T)
        att = jax.nn.softmax(att, axis=1)
        agg = jnp.einsum('bk,koihwc->boihwc', att, dft_weight)
        cw = agg[..., 0] + 1j * agg[..., 1]
        kernels = jnp.fft.ifft2(cw, axes=(-2, -1), norm='ortho').real
        kernels = jnp.clip(kernels, -10.0, 10.0)
        xr = x.reshape(1, b * cin, h, w)
        kr = kernels.reshape(b * cout, cin, KH, KW)
        out = lax.conv_general_dilated(xr, kr, window_strides=(1, 1), padding=[(1, 1), (1, 1)], dimension_numbers=('NCHW', 'OIHW', 'NCHW'), feature_group_count=b)
        out = out.reshape(b, cout, h, w) + bias[None, :, None, None]
        out = out * fbm_scale
        return out

    def _gn(v, G=32, eps=1e-05):
        B_, C_, H_, W_ = v.shape
        g = v.reshape(B_, G, C_ // G, H_, W_)
        m = jnp.mean(g, axis=(2, 3, 4), keepdims=True)
        s = jnp.var(g, axis=(2, 3, 4), keepdims=True)
        return ((g - m) / jnp.sqrt(s + eps)).reshape(v.shape)

    def _ln_c(v, eps=1e-06):
        m = jnp.mean(v, axis=1, keepdims=True)
        s = jnp.var(v, axis=1, keepdims=True)
        return (v - m) / jnp.sqrt(s + eps)

    def _ln_t(v, eps=1e-05):
        m = jnp.mean(v, axis=-1, keepdims=True)
        s = jnp.var(v, axis=-1, keepdims=True)
        return (v - m) / jnp.sqrt(s + eps)

    def _to_tokens(v):
        B_, C_, H_, W_ = v.shape
        return v.reshape(B_, C_, H_ * W_).transpose(0, 2, 1)

    def _from_tokens(t, like):
        B_, C_, H_, W_ = like.shape
        return t.transpose(0, 2, 1).reshape(B_, C_, H_, W_)
    x = x + _L0_conv_ref(_gn(x), L0_conv_weight, L0_conv_fc_w, L0_conv_fc_b)
    x = x + _L1_conv_ref(_gn(x), L1_conv_dft_weight, L1_conv_ksm_w, L1_conv_bias, L1_conv_fbm_scale)
    return x

_drawn_inputs = setup_inputs


def setup_inputs(seed=0):
    import zlib

    import numpy as np

    out = dict(_drawn_inputs(seed))
    spreads = {'L0_conv_fc_b': (0.0, 0.1), 'L1_conv_bias': (0.0, 0.1), 'L1_conv_fbm_scale': (1.0, 0.2)}
    factors = {}
    for name, (base, spread) in spreads.items():
        noise = np.random.default_rng([zlib.crc32(name.encode()), seed]).standard_normal(out[name].shape)
        drawn = base * np.exp(spread * noise) if base else spread * noise
        out[name] = jnp.asarray(drawn.astype(out[name].dtype))
    for name, factor in factors.items():
        out[name] = (out[name] * factor).astype(out[name].dtype)
    return out
```

```python
from contextlib import ExitStack

import numpy as np
import concourse.bass as bass
from concourse import mybir

F32 = mybir.dt.float32
ALU = mybir.AluOpType
ACT = mybir.ActivationFunctionType
AX_X = mybir.AxisListType.X

B, C, H, W = 8, 32, 64, 64
M1 = 32
NPIX = H * W
EPS = 1e-5
K_NUM = 16
CLIP = 10.0
CHUNKS = 4
CC = C // CHUNKS
SLOTS = 3
BD_SLOTS = 2
WP = W + 2
UB = 16
SIN60 = float(np.sqrt(3.0) / 2)

CONSTS = ["fwd_h", "fwd_cos", "fwd_sin", "fwd_nsin", "inv_re", "inv_im", "inv_w", "same_c"]
MASK4 = 128 * len(CONSTS)
HALF2 = MASK4 + 4
NCONST = HALF2 + 2
P_FC, P_KSM, P_FCB, P_BIAS, P_SCALE = 0, 32, 48, 49, 50
NPARAM = 51


def constants():
    th = 2 * np.pi / H
    m = np.arange(M1)
    h = np.arange(H) - (H - 1) / 2
    half = np.arange(W // 2) + 0.5
    out = np.zeros((128, NCONST), np.float64)

    def put(name, a):
        k = 128 * CONSTS.index(name)
        out[:, k:k + 128] = a.reshape(128, 128)

    a = np.zeros((2, H, 2, 2, 8, 4))
    for p in range(2):
        for mg in range(4):
            t = th * np.outer(h, 8 * mg + np.arange(8))
            a[p, :, p, 0, :, mg] = np.cos(t)
            a[p, :, p, 1, :, mg] = -np.sin(t)
    put("fwd_h", a)
    for name, f in (("fwd_cos", np.cos), ("fwd_sin", np.sin), ("fwd_nsin", lambda t: -np.sin(t))):
        a = np.zeros((4, W // 2, 4, M1))
        for q in range(4):
            a[q, :, q, :] = f(th * np.outer(half, m))
        put(name, a)
    for name, (fr, fi) in (("inv_re", (np.cos, lambda t: -np.sin(t))), ("inv_im", (np.sin, np.cos))):
        a = np.zeros((2, 8, 4, 2, 2, H))
        for x in range(2):
            for ml in range(8):
                for mg in range(4):
                    t = th * (8 * mg + ml) * h
                    a[x, ml, mg, 0, x] = fr(t)
                    a[x, ml, mg, 1, x] = fi(t)
        put(name, a)
    a = np.zeros((2, 2, M1, 2, W))
    weight = np.where(m == 0, 1.0, 2.0)[:, None] / NPIX
    for y in range(2):
        a[0, y, :, y] = weight * np.cos(th * np.outer(m, h))
        a[1, y, :, y] = -weight * np.sin(th * np.outer(m, h))
    put("inv_w", a)
    put("same_c", np.tile(np.eye(32), (4, 4)))
    for j in range(4):
        out[32 * j:32 * j + 32, MASK4 + j] = 1
    for p in range(2):
        out[64 * p:64 * p + 64, HALF2 + p] = 1
    return out.astype(np.float32)


def spectral_then_attention_conv(nc, x, w_modes, dft_w, params, consts, out):
    with ExitStack() as ctx:
        def sb(name, n):
            return ctx.enter_context(nc.sbuf_tensor(name, [128, n], F32))

        def sem(name):
            return ctx.enter_context(nc.semaphore(name))

        cst = sb("cst", NCONST)
        prm = sb("prm", NPARAM)
        x_buf = sb("x_buf", 4 * C * W)
        fold_buf = sb("fold_buf", 8192)
        y_buf = sb("y_buf", B * UB * WP)
        w_buf = sb("w_buf", B * (UB + 1) * WP)
        bd_buf = sb("bd_buf", BD_SLOTS * M1 * 64)
        q_buf = sb("q_buf", 4096)
        sq_trash, att_diag, spread_att = q_buf[:, 0:2048], q_buf[:, 2048:2560], q_buf[:, 2560:3072]
        r_buf = sb("r_buf", 4096)
        taps = sb("taps", 4 * 9 * 32)
        conv_w = [sb(f"conv_w{r}", B * 3 * 32) for r in range(2)]
        fc_diag = sb("fc_diag", 128)
        sums1 = sb("sums1", 2 * 4 * 32)
        stat1 = sb("stat1", 8 * 7)
        bconst = sb("bconst", 2)
        kern = sb("kern", 3 * 288 + 32)
        st2 = sb("st2", 160)

        def const(name):
            k = 128 * CONSTS.index(name)
            return cst[:, k:k + 128]

        mask4 = cst[:, MASK4:MASK4 + 4]
        ones2 = cst[:, HALF2:HALF2 + 2]
        eye32 = const("same_c")[:, 0:32]

        xh = x_buf[:].rearrange("p (q c w) -> p q c w", q=4, c=C)
        xr = x_buf[:].rearrange("p (b u w) -> p b u w", b=B, u=UB)
        fold = fold_buf[:].rearrange("p (c e q w) -> p c e q w", c=C, e=2, q=4)
        t_rows = fold_buf[:].rearrange("p (g x h c) -> p g x h c", g=2, x=2, c=C)
        dft_sb = fold_buf[:, 0:2304]
        dft_v = fold_buf[:, 2304:4608].rearrange("p (r u v k) -> p r u v k", r=2, u=3, v=3)
        dft_t = fold_buf[:, 4608:4608 + 4 * 384].rearrange("p (t n) -> p t n", t=4)
        y_rows = y_buf[:, 0:8192].rearrange("p (e f c) -> p e f c", e=2, c=C)
        xa = y_buf[:].rearrange("p (b u w) -> p b u w", b=B, u=UB)
        xb = w_buf[:].rearrange("p (b u w) -> p b u w", b=B, u=UB + 1)
        modes = w_buf[:, 0:8192].rearrange("p (o ml n) -> p o ml n", o=32, ml=8)
        bd = bd_buf[:].rearrange("p (s n b g r) -> p s n b g r", s=BD_SLOTS, n=M1, b=B, g=4)
        ost = bd_buf[:, 0:2048].rearrange("p (s n) -> p s n", s=2)
        sq = q_buf[:].rearrange("p (s q c w) -> p s q c w", s=2, q=4, c=CC)
        mixed = q_buf[:].rearrange("p (nl b ml g) -> p nl b ml g", nl=8, b=B, ml=8)
        r_modes = r_buf[:].rearrange("p (g o y n) -> p g o y n", g=2, y=2, o=32)
        tap = taps[:].rearrange("p (k t i) -> p k t i", k=4, t=9)
        cw = [t[:].rearrange("p (b k o) -> p b k o", b=B, k=3) for t in conv_w]
        s1v = sums1[:].rearrange("p (s q c) -> p s q c", s=2, q=4)
        mean1, msq1, var1, std1, rstd1, dc1, tmp1 = (stat1[:, 8 * k:8 * k + 8] for k in range(7))

        part1 = st2[:, 0:16].rearrange("p (b s) -> p b s", s=2)
        comb = st2[:, 16:32].rearrange("p (g s b) -> p g s b", g=2, s=2)
        names = ["mean", "msq", "var", "std", "rstd", "pool", "mdiag", "rdiag", "btot", "t"]
        g2 = {k: st2[:, 32 + 8 * i:40 + 8 * i].rearrange("p (g b) -> p g b", g=2) for i, k in enumerate(names)}
        att_s = st2[:, 112:144].rearrange("p (g k b) -> p g k b", g=2, k=4)
        soft = sb("soft", 2 * 96)
        last_word = sb("last_word", 2)[:]

        slot = [ctx.enter_context(nc.psum_tensor(f"slot{i}", [128, 1024], F32)) for i in range(SLOTS)]
        small = ctx.enter_context(nc.psum_tensor("small", [128, 512], F32))
        aggp = ctx.enter_context(nc.psum_tensor("aggp", [128, 512], F32))

        fwd_h_in = sem("fwd_h_in"); cst_in = sem("cst_in"); prm_in = sem("prm_in")
        xh_in = [sem(f"xh_in{k}") for k in range(CHUNKS)]
        modes_in = [sem(f"modes_in{k}") for k in range(2)]
        xr_in = [sem(f"xr_in{k}") for k in range(4)]; dft_in = sem("dft_in"); stored = [sem(f"stored{k}") for k in range(2)]
        f1_done = sem("f1_done"); stat_done = sem("stat_done"); f2_done = sem("f2_done")
        mix_done = sem("mix_done"); fc_done = sem("fc_done"); i1_done = sem("i1_done")
        i2_done = sem("i2_done"); small_done = sem("small_done"); agg_done = sem("agg_done")
        conv_done = sem("conv_done"); bias_done = sem("bias_done")
        sq_ready = sem("sq_ready"); y_ready = sem("y_ready"); std_ready = sem("std_ready")
        mixed_ready = sem("mixed_ready"); r_act = sem("r_act"); t_act = sem("t_act")
        sq2_ready = sem("sq2_ready"); std2_ready = sem("std2_ready"); exp_ready = sem("exp_ready")
        w1_ready = sem("w1_ready"); out_ready = sem("out_ready")
        fold_ready = sem("fold_ready"); sq_used = sem("sq_used"); sums_ready = sem("sums_ready")
        var_ready = sem("var_ready"); bd_ready = sem("bd_ready"); fcd_ready = sem("fcd_ready")
        r_dve = sem("r_dve"); t_dve = sem("t_dve"); xa_ready = sem("xa_ready"); xb_ready = sem("xb_ready")
        chain_ready = sem("chain_ready"); kern_ready = sem("kern_ready"); conv_ready = sem("conv_ready")
        att_ready = sem("att_ready"); w0_ready = sem("w0_ready"); pads_ready = sem("pads_ready")
        dve = sem("dve_done")
        bd_zero = sem("bd_zero"); w_zero = sem("w_zero"); pool = sem("pool_done"); taps_ready = sem("taps_ready")

        users = [("f1", k) for k in range(8)] + [("f2", 0), ("f2", 1)]
        for m in range(8):
            users += [("mix", m)] + ([("f2", m + 2)] if m + 2 < 8 else [])
        users += [("fc", k) for k in range(4)]
        users += [("i1", k) for k in range(4)] + [("i1", 4)] + [("i2", k) for k in range(4)]
        users += [("i1", k) for k in range(5, 8)] + [("i2", k) for k in range(4, 8)]
        users += [("conv", b) for b in range(B)]
        slot_of = {u: n % SLOTS for n, u in enumerate(users)}
        freed = {"f1": lambda k: [(y_ready, k + 1)],
                 "f2": lambda k: [(bd_ready, k + 1)],
                 "mix": lambda k: [(mixed_ready, k + 1)],
                 "fc": lambda k: [(r_act, 2 * (k + 1)), (r_dve, 2 * (k + 1))],
                 "i1": lambda k: [(t_act, k + 1), (t_dve, k + 1)],
                 "i2": lambda k: [(xa_ready, 2 * (k + 1))],
                 "conv": lambda k: [(out_ready, k + 1)]}

        def take_slot(pe, user):
            n = users.index(user)
            if n >= SLOTS:
                stage, k = users[n - SLOTS]
                for s, v in freed[stage](k):
                    pe.wait_ge(s, v)
            return slot[slot_of[user]]

        def turned(k, half, g):
            dst = r_modes[:, g].rearrange("p o y (nq nl) -> p y nq o nl", nq=4)[:, :, :, :, 2 * k + half]
            c0 = 512 * half + 256 * g
            return dst, slot[slot_of["fc", k]][:, c0:c0 + 256].rearrange("p (y q o) -> p y q o", y=2, q=4)

        def rows(k, half):
            g, c0 = k // 4, 8 * (k % 4) + 4 * half
            dst = t_rows[:, g, :, :, c0:c0 + 4].rearrange("p x h c -> p c x h")
            return dst, slot[slot_of["i1", k]][:, 512 * half:512 * half + 512].rearrange("p (c x h) -> p c x h", c=4, x=2)

        block = ctx.enter_context(nc.Block())

        @block.sync
        def _(sp):
            sp.dma_start(cst[:, 0:128], consts[:, 0:128]).then_inc(fwd_h_in, 16)
            for k in range(CHUNKS):
                for b in range(B):
                    p, q = divmod(b, 4)
                    sp.dma_start(xh[64 * p:64 * p + 64, q, CC * k:CC * k + CC, :],
                                 x[b, CC * k:CC * k + CC].rearrange("c h w -> h c w")).then_inc(xh_in[k], 16)
                if k == 0:
                    sp.dma_start(cst[:, 128:NCONST], consts[:, 128:NCONST]).then_inc(cst_in, 16)
                    for j in range(4):
                        sp.dma_start(prm[32 * j:32 * j + 32, :], params).then_inc(prm_in, 16)
            for k in range(2):
                for mg in range(4):
                    m0 = 8 * mg + 4 * k
                    sp.dma_start(modes[32 * mg:32 * mg + 32, :, 4 * k:4 * k + 4, :].rearrange("i o m n -> i o (m n)"),
                                 w_modes[0, :, :, m0:m0 + 4, :].rearrange("i o m n -> i o (m n)")).then_inc(modes_in[k], 16)
            sp.wait_ge(f1_done, 16)
            sp.wait_ge(sums_ready, CHUNKS)
            sp.dma_start(dft_sb.rearrange("p (k n) -> p k n", k=4),
                         dft_w.rearrange("(kg kl) o i kh kw z -> (kl o) kg (i kh kw z)", kg=4)).then_inc(dft_in, 16)
            sp.wait_ge(fold_ready, 2 * CHUNKS)
            sp.wait_ge(sq_ready, CHUNKS)
            for b in (0, 2, 1, 3, 4, 6, 5, 7):
                for j in range(4):
                    sp.dma_start(xr[32 * j:32 * j + 32, b],
                                 x[b].rearrange("c (u j) w -> j c u w", j=4)[j]).then_inc(xr_in[2 * (b // 4) + b % 2], 16)
            for b in range(B):
                sp.wait_ge(out_ready, b + 1)
                for j in range(4):
                    sp.dma_start(out[b].rearrange("c (u j) w -> j c u w", j=4)[j],
                                 ost[32 * j:32 * j + 32, b % 2, :].rearrange("c (u w) -> c u w", w=W)
                                 ).then_inc(stored[b % 2], 16)
            for k in range(2):
                sp.wait_ge(stored[k], 16 * 4 * (B // 2))

        @block.gpsimd
        def _(gp):
            nc.gpsimd.memset(bd_buf[:], 0.0).then_inc(bd_zero, 1)
            gp.wait_ge(bd_zero, 1)
            nc.gpsimd.memset(conv_w[0][96:128, :], 0.0).then_inc(w_zero, 1)
            gp.wait_ge(w_zero, 1)
            nc.gpsimd.memset(conv_w[1][0:32, :], 0.0).then_inc(w_zero, 1)

            gp.wait_ge(dft_in, 16)
            gp.wait_ge(w_zero, 2)
            a = dft_sb.rearrange("p (k u v z) -> p z v u k", u=3, v=3, z=2)
            steps = 0

            def step(ins):
                nonlocal steps
                steps += 1
                ins.then_inc(pool, 1)
                gp.wait_ge(pool, steps)

            def tt(o, p, q, op):
                step(nc.gpsimd.tensor_tensor(o, p, q, op))

            def scaled(o, p, f):
                step(nc.gpsimd.tensor_scalar(o, p, f, None, ALU.mult))

            def n3(t):
                return dft_t[:, t, :].rearrange("p (u k) -> p u k", u=3)

            for z in range(2):
                tt(n3(z), a[:, z, 1], a[:, z, 2], ALU.add)
                tt(n3(2 + z), a[:, z, 1], a[:, z, 2], ALU.subtract)
            for z in range(2):
                tt(dft_v[:, z, :, 0], a[:, z, 0], n3(z), ALU.add)
            for z in range(2):
                scaled(n3(z), n3(z), -0.5)
                scaled(n3(2 + z), n3(2 + z), SIN60)
            for z in range(2):
                tt(n3(z), n3(z), a[:, z, 0], ALU.add)
            for z, first, second in ((0, ALU.subtract, ALU.add), (1, ALU.add, ALU.subtract)):
                tt(dft_v[:, z, :, 1], n3(z), n3(3 - z), first)
                tt(dft_v[:, z, :, 2], n3(z), n3(3 - z), second)
            re, im = dft_v[:, 0], dft_v[:, 1]

            def row(kh):
                return tap[:, :, 3 * kh:3 * kh + 3, :].rearrange("p k t i -> p t k i")

            def by_kernel(t):
                return t.rearrange("p v (k i) -> p v k i", k=4)

            tt(n3(0), re[:, 1], re[:, 2], ALU.add)
            tt(n3(1), im[:, 1], im[:, 2], ALU.subtract)
            tt(row(0), by_kernel(re[:, 0]), by_kernel(n3(0)), ALU.add)
            scaled(n3(2), n3(0), -0.5)
            scaled(n3(1), n3(1), SIN60)
            tt(n3(3), n3(2), re[:, 0], ALU.add)
            tt(row(1), by_kernel(n3(3)), by_kernel(n3(1)), ALU.subtract)
            tt(row(2), by_kernel(n3(3)), by_kernel(n3(1)), ALU.add)
            nc.gpsimd.memset(last_word, 0.0).then_inc(taps_ready, 1)

        @block.scalar
        def _(act):
            def copy_y(k):
                act.wait_ge(f1_done, 2 * k + 2)
                act.activation(y_rows[:, :, :, 4 * k:4 * k + 4].rearrange("p e f c -> p c e f"),
                               slot[slot_of["f1", k]][:].rearrange("p (c e f) -> p c e f", c=4, e=2),
                               ACT.Copy).then_inc(y_ready, 1)

            for k in range(CHUNKS):
                act.wait_ge(xh_in[k], 16 * B)
                if k >= 2:
                    act.wait_ge(sq_used, k - 1)
                act.activation(sq[:, k % 2], xh[:, :, CC * k:CC * k + CC, :], ACT.Square).then_inc(sq_ready, 1)
                copy_y(2 * k)
                copy_y(2 * k + 1)
            act.wait_ge(var_ready, 1)
            act.activation(std1, var1, ACT.Sqrt).then_inc(std_ready, 1)
            for ml in range(8):
                act.wait_ge(mix_done, ml + 1)
                act.activation(mixed[:, :, :, ml, :], slot[slot_of["mix", ml]][:, 0:512].rearrange(
                    "p (nl b g) -> p nl b g", nl=8, b=B), ACT.Copy).then_inc(mixed_ready, 1)
            for k in range(4):
                act.wait_ge(fc_done, 2 * k + 1)
                for g in range(2):
                    act.activation(*turned(k, 0, g), ACT.Copy).then_inc(r_act, 1)

            def copy_t(k):
                act.wait_ge(i1_done, 2 * k + 1)
                if k == 0:
                    act.wait_ge(taps_ready, 1)
                act.activation(*rows(k, 0), ACT.Copy).then_inc(t_act, 1)

            def squares(b, n):
                if n >= 2:
                    act.wait_ge(sq2_ready, n - 1)
                act.activation(sq_trash[:, 1024 * (n % 2):1024 * (n % 2) + 1024].rearrange("p (u w) -> p u w", u=UB), xa[:, b, :, 1:W + 1], ACT.Square,
                               accum_out=comb[:, b // 4, 1, b % 4:b % 4 + 1]).then_inc(sq2_ready, 1)

            def finish_stats(g):
                act.wait_ge(chain_ready, 5 * g + 2)
                act.activation(g2["std"][:, g], g2["var"][:, g], ACT.Sqrt).then_inc(std2_ready, 1)

            def softmax(g):
                z = soft[0:4, 96 * g:96 * g + 96]
                act.wait_ge(small_done, 3 * g + 2)
                act.activation(z[:, 0:16], small[0:4, 64:80], ACT.Exp, scale=-1.0 / NPIX).then_inc(exp_ready, 1)
                act.wait_ge(chain_ready, 5 * g + 4)
                act.activation(z[:, 48:64], z[:, 32:48], ACT.Exp, bias=z[:, 81:82],
                               accum_out=z[:, 82:83]).then_inc(exp_ready, 1)

            def weights(g):
                act.wait_ge(kern_ready, g + 1)
                kt = kern[:, 576:864]
                for i in range(4):
                    for kh in range(3):
                        j = kh + 1
                        act.activation(conv_w[1][32 * j:32 * j + 32, 96 * (4 * g + i):96 * (4 * g + i) + 96],
                                       kt[32 * i:32 * i + 32, 96 * kh:96 * kh + 96], ACT.Copy).then_inc(w1_ready, 1)

            def out_copy(b):
                act.wait_ge(conv_done, b + 1)
                if b >= 2:
                    act.wait_ge(stored[b % 2], 64 * (b // 2))
                g = b // 4
                act.activation(ost[:, b % 2, :], slot[slot_of["conv", b]][:], ACT.Identity,
                               bias=g2["btot"][:, g, b % 4:b % 4 + 1]).then_inc(out_ready, 1)

            for k in range(5):
                copy_t(k)
            for x in range(2):
                act.wait_ge(xa_ready, 4 * x + 4)
                for y in range(2):
                    squares(2 * y + x, 2 * x + y)
            copy_t(5)
            finish_stats(0)
            copy_t(6)
            softmax(0)
            copy_t(7)
            for x in range(2):
                act.wait_ge(xa_ready, 8 + 4 * x + 4)
                for y in range(2):
                    squares(4 + 2 * y + x, 4 + 2 * x + y)
                if x == 0:
                    weights(0)
            finish_stats(1)
            act.wait_ge(conv_ready, 1)
            out_copy(0)
            softmax(1)
            out_copy(1)
            out_copy(2)
            weights(1)
            for b in range(3, B):
                if b == 4:
                    act.wait_ge(conv_ready, 2)
                out_copy(b)

        @block.vector
        def _(v):
            done = 0

            def chain(ins):
                nonlocal done
                done += 1
                ins.then_inc(dve, 1)
                v.wait_ge(dve, done)

            for k in range(CHUNKS):
                cs = slice(CC * k, CC * k + CC)
                v.wait_ge(xh_in[k], 16 * B)
                right, left = xh[:, :, cs, 32:64], xh[:, :, cs, 31::-1]
                for e, op in ((0, ALU.add), (1, ALU.subtract)):
                    nc.vector.tensor_tensor(fold[:, cs, e].rearrange("p c q w -> p q c w"), right, left,
                                            op).then_inc(fold_ready, 1)
                v.wait_ge(fold_ready, 2 * k + 1)
                nc.vector.tensor_reduce(s1v[:, 0, :, cs], fold[:, cs, 0].rearrange("p c q w -> p q c w"), AX_X,
                                        ALU.add).then_inc(sums_ready, 1)
                v.wait_ge(sq_ready, k + 1)
                nc.vector.tensor_reduce(s1v[:, 1, :, cs], sq[:, k % 2], AX_X, ALU.add).then_inc(sq_used, 1)

            v.wait_ge(prm_in, 64)
            v.wait_ge(cst_in, 16)
            nc.vector.tensor_tensor(fc_diag[:].rearrange("p (q o) -> p q o", q=4),
                                    prm[:, P_FC:P_FC + 32].unsqueeze(1).broadcast_to([128, 4, 32]),
                                    mask4.unsqueeze(2).broadcast_to([128, 4, 32]),
                                    ALU.mult).then_inc(fcd_ready, 1)
            chain(nc.vector.tensor_tensor(bconst[:, 0:1], prm[:, P_BIAS:P_BIAS + 1], prm[:, P_SCALE:P_SCALE + 1], ALU.mult))
            chain(nc.vector.tensor_tensor(bconst[:, 0:1], bconst[:, 0:1], prm[:, P_FCB:P_FCB + 1], ALU.add))

            v.wait_ge(stat_done, 1)
            sp_ = small[:, 0:16].rearrange("p (s q p2) -> p s p2 q", s=2, q=4)
            nc.vector.tensor_scalar(mean1.rearrange("p (a b) -> p a b", a=2), sp_[:, 0], 1.0 / NPIX, None, ALU.mult)
            chain(nc.vector.tensor_scalar(msq1.rearrange("p (a b) -> p a b", a=2), sp_[:, 1], 1.0 / NPIX, EPS, ALU.mult, ALU.add))
            chain(nc.vector.tensor_tensor(tmp1, mean1, mean1, ALU.mult))
            nc.vector.tensor_tensor(var1, msq1, tmp1, ALU.subtract).then_inc(var_ready, 1)
            v.wait_ge(std_ready, 1)
            chain(nc.vector.reciprocal(rstd1, std1))
            chain(nc.vector.scalar_tensor_tensor(out=dc1, in0=mean1, scalar=float(NPIX), in1=rstd1, op0=ALU.mult, op1=ALU.mult))

            v.wait_ge(bd_zero, 1)
            for ml in range(8):
                v.wait_ge(f2_done, ml + 1)
                if ml >= BD_SLOTS:
                    v.wait_ge(mix_done, ml - BD_SLOTS + 1)
                z = slot[slot_of["f2", ml]][:, 0:512].rearrange("p (r b n) -> p r b n", r=2, b=B)
                for mg in range(4):
                    ps = slice(32 * mg, 32 * mg + 32)
                    ins = nc.vector.tensor_tensor(
                        bd[ps, ml % BD_SLOTS, :, :, mg, :].rearrange("p n b r -> p r b n"), z[ps],
                        rstd1[ps].unsqueeze(1).unsqueeze(3).broadcast_to([32, 2, B, M1]), ALU.mult)
                    if ml == 0 and mg == 0:
                        chain(ins)
                        ins = nc.vector.tensor_tensor(bd[0:32, 0, 0, :, 0, 0], bd[0:32, 0, 0, :, 0, 0], dc1[0:32], ALU.subtract)
                        chain(ins)
                ins.then_inc(bd_ready, 1)

            for k in range(4):
                v.wait_ge(fc_done, 2 * k + 2)
                for g in range(2):
                    nc.vector.tensor_copy(*turned(k, 1, g)).then_inc(r_dve, 1)

            def copy_t(k):
                v.wait_ge(i1_done, 2 * k + 2)
                if k == 0:
                    v.wait_ge(taps_ready, 1)
                nc.vector.tensor_copy(*rows(k, 1)).then_inc(t_dve, 1)

            def add_x(k):
                g, x, u0 = k // 4, (k // 2) % 2, 8 * (k % 2)
                v.wait_ge(i2_done, k + 1)
                ps = slot[slot_of["i2", k]][:].rearrange("p (u y w) -> p u y w", u=8, y=2)
                for y in range(2):
                    b = 4 * g + 2 * y + x
                    nc.vector.scalar_tensor_tensor(
                        out=xa[:, b, u0:u0 + 8, 1:W + 1], in0=ps[:, :, y, :], scalar=mean1[:, b:b + 1],
                        in1=xr[:, b, u0:u0 + 8, :], op0=ALU.subtract, op1=ALU.add,
                        accum_out=part1[:, b, k % 2:k % 2 + 1]).then_inc(xa_ready, 1)

            def shift(b, count):
                v.wait_ge(xa_ready, count)
                nc.vector.tensor_copy(xb[0:64, b, 1:UB + 1, 1:W + 1], xa[64:128, b, :, 1:W + 1]).then_inc(xb_ready, 1)
                nc.vector.tensor_copy(xb[64:128, b, 0:UB, 1:W + 1], xa[0:64, b, :, 1:W + 1]).then_inc(xb_ready, 1)

            def bcast(ap, *shape):
                whole = list(ap.shape) + list(shape)
                for _ in shape:
                    ap = ap.unsqueeze(len(ap.shape))
                return ap.broadcast_to(whole)

            def chain_a(g):
                bs = slice(4 * g, 4 * g + 4)
                nc.vector.tensor_tensor(comb[:, g, 0, :], part1[:, bs, 0], part1[:, bs, 1], ALU.add).then_inc(chain_ready, 1)

            def chain_b(g):
                v.wait_ge(small_done, 3 * g + 1)
                nc.vector.tensor_scalar(g2["mean"][:, g], small[:, 32:36], 1.0 / NPIX, None, ALU.mult)
                chain(nc.vector.tensor_scalar(g2["msq"][:, g], small[:, 36:40], 1.0 / NPIX, EPS, ALU.mult, ALU.add))
                chain(nc.vector.tensor_tensor(g2["t"][:, g], g2["mean"][:, g], g2["mean"][:, g], ALU.mult))
                nc.vector.tensor_tensor(g2["var"][:, g], g2["msq"][:, g], g2["t"][:, g], ALU.subtract).then_inc(chain_ready, 1)

            def chain_c(g):
                v.wait_ge(std2_ready, g + 1)
                nc.vector.reciprocal(g2["rstd"][:, g], g2["std"][:, g])
                chain(nc.vector.scalar_tensor_tensor(out=g2["t"][:, g], in0=g2["mean"][:, g], scalar=-float(NPIX // 4),
                                                     in1=comb[:, g, 0, :], op0=ALU.mult, op1=ALU.add))
                nc.vector.tensor_tensor(g2["pool"][:, g], g2["t"][:, g], g2["rstd"][:, g], ALU.mult).then_inc(chain_ready, 1)
                chain(nc.vector.tensor_tensor(g2["rdiag"][:, g], g2["rstd"][:, g], mask4, ALU.mult))
                nc.vector.tensor_tensor(g2["mdiag"][:, g], g2["mean"][:, g], mask4, ALU.mult)
                chain(nc.vector.tensor_reduce(bconst[:, 1:2], g2["rdiag"][:, g], AX_X, ALU.add))

            def chain_d(g):
                z = soft[0:4, 96 * g:96 * g + 96]
                v.wait_ge(exp_ready, 2 * g + 1)
                chain(nc.vector.tensor_scalar(z[:, 16:32], z[:, 0:16], 1.0, None, ALU.add))
                chain(nc.vector.reciprocal(z[:, 32:48], z[:, 16:32]))
                chain(nc.vector.tensor_reduce(z[:, 80:81], z[:, 32:48], AX_X, ALU.max))
                nc.vector.tensor_scalar(z[:, 81:82], z[:, 80:81], -1.0, None, ALU.mult).then_inc(chain_ready, 1)
                v.wait_ge(exp_ready, 2 * g + 2)
                chain(nc.vector.reciprocal(z[:, 83:84], z[:, 82:83]))
                nc.vector.tensor_scalar(spread_att[0:4].rearrange("b (k o) -> b k o", k=K_NUM),
                                        z[:, 48:64].unsqueeze(2).broadcast_to([4, K_NUM, 32]), z[:, 83:84], None,
                                        ALU.mult).then_inc(chain_ready, 1)

            def chain_e(g):
                v.wait_ge(small_done, 3 * g + 3)
                chain(nc.vector.tensor_copy(att_s[:, g], small[:, 128:144].rearrange("p (k b) -> p k b", k=4)))
                nc.vector.tensor_tensor(
                    att_diag.rearrange("p (b k o) -> p b k o", b=4, k=4),
                    eye32.unsqueeze(1).unsqueeze(1).broadcast_to([128, 4, 4, 32]),
                    att_s[:, g].rearrange("p k b -> p b k").unsqueeze(3).broadcast_to([128, 4, 4, 32]),
                    ALU.mult).then_inc(att_ready, 1)

            def chain_f(g):
                k0, k1, kt, ks = kern[:, 0:288], kern[:, 288:576], kern[:, 576:864], kern[:, 864:896]
                v.wait_ge(agg_done, g + 1)
                chain(nc.vector.tensor_scalar(k0, aggp[:, 0:288], 1.0 / 3.0, CLIP, ALU.mult, ALU.min))
                chain(nc.vector.tensor_scalar(k1, k0, -CLIP, prm[:, P_SCALE:P_SCALE + 1], ALU.max, ALU.mult))
                chain(nc.vector.transpose(k0, k1))
                if g:
                    v.wait_ge(w1_ready, 12 * g)
                chain(nc.vector.tensor_scalar(kt, k0, bconst[:, 1:2], None, ALU.mult))
                chain(nc.vector.tensor_reduce(ks, kt.rearrange("p (t o) -> p o t", t=9), AX_X, ALU.add))
                nc.vector.tensor_tensor(kt[:, 128:160], kt[:, 128:160], eye32, ALU.add).then_inc(kern_ready, 1)
                v.wait_ge(kern_ready, g + 1)
                for i in range(4):
                    for kh in range(3):
                        ins = nc.vector.tensor_copy(conv_w[0][32 * kh:32 * kh + 32, 96 * (4 * g + i):96 * (4 * g + i) + 96],
                                                    kt[32 * i:32 * i + 32, 96 * kh:96 * kh + 96])
                ins.then_inc(w0_ready, 1)

            def pads(g):
                bs = slice(4 * g, 4 * g + 4)
                mean = g2["mean"][:, g]
                nc.vector.tensor_copy(xa[:, bs, :, 0:WP:WP - 1], bcast(mean, UB, 2))
                nc.vector.tensor_copy(xb[:, bs, :, 0:WP:WP - 1], bcast(mean, UB + 1, 2))
                nc.vector.tensor_copy(xb[0:64, bs, 0, 1:W + 1], bcast(mean[0:64], W))
                nc.vector.tensor_copy(xb[64:128, bs, UB, 1:W + 1], bcast(mean[64:128], W)).then_inc(pads_ready, 1)

            def bias_total(g):
                bs = slice(4 * g, 4 * g + 4)
                v.wait_ge(bias_done, g + 1)
                nc.vector.scalar_tensor_tensor(out=g2["btot"][:, g], in0=mean1[:, bs], scalar=bconst[:, 0:1],
                                               in1=small[:, 160:164], op0=ALU.add, op1=ALU.subtract).then_inc(conv_ready, 1)

            for k in range(5):
                copy_t(k)
            for x in range(2):
                v.wait_ge(xr_in[x], 128)
                add_x(2 * x)
                add_x(2 * x + 1)
                if x == 1:
                    v.wait_ge(xa_ready, 8)
                    chain_a(0)
                for y in range(2):
                    shift(2 * y + x, 4 * x + 4)
            copy_t(5)
            chain_b(0)
            copy_t(6)
            chain_c(0)
            pads(0)
            copy_t(7)
            chain_d(0)
            v.wait_ge(xr_in[2], 128)
            add_x(4)
            add_x(5)
            chain_e(0)
            for y in range(2):
                shift(4 + 2 * y, 12)
            v.wait_ge(xr_in[3], 128)
            add_x(6)
            chain_f(0)
            add_x(7)
            bias_total(0)
            v.wait_ge(xa_ready, 16)
            chain_a(1)
            chain_b(1)
            chain_c(1)
            for y in range(2):
                shift(5 + 2 * y, 16)
            pads(1)
            chain_d(1)
            chain_e(1)
            chain_f(1)
            bias_total(1)

        @block.tensor
        def _(pe):
            def f1(k):
                ps = take_slot(pe, ("f1", k))
                for half in range(2):
                    for i in range(4):
                        c, e = 4 * k + 2 * half + i // 2, i % 2
                        last = pe.matmul(ps[:, 512 * half + 128 * i:512 * half + 128 * i + 128],
                                         fold[:, c, e].rearrange("p q w -> p (q w)"), const("fwd_h"), start=True, stop=True)
                    last.then_inc(f1_done, 1)

            def f2(ml):
                ps = take_slot(pe, ("f2", ml))

                def y(e, p, r):
                    f = 64 * p + 32 * r + 4 * ml
                    return y_rows[:, e, f:f + 4, :].rearrange("w g c -> w (g c)")

                for p in range(2):
                    re, im = ps[:, 128 * p:128 * p + 128], ps[:, 256 + 128 * p:384 + 128 * p]
                    pe.matmul(re, y(0, p, 0), const("fwd_cos"), start=True, stop=False)
                    pe.matmul(re, y(1, p, 1), const("fwd_sin"), start=False, stop=True)
                    pe.matmul(im, y(0, p, 1), const("fwd_cos"), start=True, stop=False)
                    last = pe.matmul(im, y(1, p, 0), const("fwd_nsin"), start=False, stop=True)
                last.then_inc(f2_done, 1)

            def mix(ml):
                ps = take_slot(pe, ("mix", ml))
                pe.wait_ge(bd_ready, ml + 1)
                if ml % 4 == 0:
                    pe.wait_ge(modes_in[ml // 4], 64)
                for nl in range(8):
                    for nq in range(4):
                        n = 8 * nq + nl
                        last = pe.matmul(ps[32 * nq:32 * nq + 32, 64 * nl:64 * nl + 64], modes[:, :, ml, n],
                                         bd[:, ml % BD_SLOTS, n].rearrange("p b g r -> p (b g r)"), start=True, stop=True)
                last.then_inc(mix_done, 1)

            def fc(k):
                ps = take_slot(pe, ("fc", k))
                for half in range(2):
                    for bb in range(4):
                        last = pe.matmul(ps[:, 512 * half + 128 * bb:512 * half + 128 * bb + 128],
                                         mixed[:, 2 * k + half, 2 * bb:2 * bb + 2].rearrange("p b m g -> p (b m g)"),
                                         fc_diag[:], start=True, stop=True)
                    last.then_inc(fc_done, 1)

            def i1(k):
                ps = take_slot(pe, ("i1", k))
                g, c0 = k // 4, 8 * (k % 4)
                for half in range(2):
                    for i in range(4):
                        for r, e in ((0, "inv_re"), (1, "inv_im")):
                            col = 512 * half + 128 * i
                            last = pe.matmul(ps[64 * r:64 * r + 64, col:col + 128], r_modes[:, g, c0 + 4 * half + i].rearrange("p y n -> p (y n)"),
                                             const(e), start=True, stop=True)
                    last.then_inc(i1_done, 1)

            def i2(k):
                ps = take_slot(pe, ("i2", k))
                g, x, u0 = k // 4, (k // 2) % 2, 8 * (k % 2)
                for u in range(8):
                    h = 4 * (u0 + u)
                    last = pe.matmul(ps[:, 128 * u:128 * u + 128],
                                     t_rows[:, g, x, h:h + 4, :].rearrange("p j c -> p (j c)"), const("inv_w"),
                                     start=True, stop=True)
                last.then_inc(i2_done, 1)

            def sum_rows(g):
                pe.wait_ge(chain_ready, 5 * g + 1)
                pe.wait_ge(sq2_ready, 4 * g + 4)
                pe.matmul(small[:, 32:40], const("same_c"), comb[:, g].rearrange("p s b -> p (s b)"),
                          start=True, stop=True).then_inc(small_done, 1)

            def logits(g):
                pe.wait_ge(chain_ready, 5 * g + 3)
                pe.matmul(small[0:4, 64:80], g2["pool"][:, g], prm[:, P_KSM:P_KSM + K_NUM], start=True,
                          stop=True).then_inc(small_done, 1)

            def spread(g):
                pe.wait_ge(chain_ready, 5 * g + 5)
                for kg in range(4):
                    last = pe.matmul(small[:, 128 + 4 * kg:132 + 4 * kg],
                                     spread_att[0:4, 128 * kg:128 * kg + 128],
                                     const("same_c")[0:4, 0:4], start=True, stop=True)
                last.then_inc(small_done, 1)

            def aggregate(g):
                pe.wait_ge(att_ready, g + 1)
                if g == 0:
                    pe.wait_ge(taps_ready, 1)
                for kg in range(4):
                    for i in range(4):
                        last = pe.matmul(aggp[32 * i:32 * i + 32, 0:288],
                                         att_diag[:, 128 * i + 32 * kg:128 * i + 32 * kg + 32],
                                         tap[:, kg].rearrange("p t i -> p (t i)"), start=(kg == 0), stop=(kg == 3))
                last.then_inc(agg_done, 1)

            def mean_through_kernels(g):
                pe.wait_ge(kern_ready, g + 1)
                for j in range(4):
                    last = pe.matmul(small[32 * j:32 * j + 32, 160:164], kern[:, 864:896], g2["mdiag"][:, g],
                                     start=True, stop=True)
                last.then_inc(bias_done, 1)

            def conv(b):
                ps = take_slot(pe, ("conv", b))
                if b % 4 == 0:
                    g = b // 4
                    pe.wait_ge(w0_ready, g + 1)
                    pe.wait_ge(w1_ready, 12 * (g + 1))
                    pe.wait_ge(w_zero, 2)
                    pe.wait_ge(pads_ready, g + 1)
                    pe.wait_ge(xb_ready, 8 * (g + 1))
                for half in range(2):
                    u0 = 8 * half
                    for kw in range(3):
                        for j, (r, src, u) in enumerate(((1, xb, u0), (0, xa, u0), (1, xa, u0), (0, xb, u0 + 1))):
                            last = pe.matmul(ps[32 * j:32 * j + 32, 512 * half:512 * half + 512], cw[r][:, b, kw, :],
                                             src[:, b, u:u + 8, kw:kw + W], start=(kw == 0), stop=(kw == 2))
                last.then_inc(conv_done, 1)

            pe.wait_ge(fwd_h_in, 16)
            for k in range(8):
                if k % 2 == 0:
                    pe.wait_ge(fold_ready, k + 2)
                f1(k)
            pe.wait_ge(cst_in, 16)
            pe.wait_ge(y_ready, 8)
            f2(0)
            pe.wait_ge(sums_ready, CHUNKS)
            pe.wait_ge(sq_used, CHUNKS)
            for s in range(2):
                for q in range(4):
                    for mg in range(4):
                        col = 8 * s + 2 * q
                        last = pe.matmul(small[32 * mg:32 * mg + 32, col:col + 2], s1v[:, s, q, :], ones2,
                                         start=True, stop=True)
            last.then_inc(stat_done, 1)
            f2(1)
            for ml in range(8):
                mix(ml)
                if ml + 2 < 8:
                    f2(ml + 2)
            pe.wait_ge(mixed_ready, 8)
            pe.wait_ge(fcd_ready, 1)
            for k in range(4):
                fc(k)
            pe.wait_ge(r_act, 8)
            pe.wait_ge(r_dve, 8)
            for k in range(5):
                i1(k)
            pe.wait_ge(t_act, 4)
            pe.wait_ge(t_dve, 4)
            for k in range(4):
                i2(k)
            i1(5)
            sum_rows(0)
            i1(6)
            logits(0)
            i1(7)
            spread(0)
            pe.wait_ge(t_act, 8)
            pe.wait_ge(t_dve, 8)
            i2(4)
            i2(5)
            i2(6)
            aggregate(0)
            i2(7)
            mean_through_kernels(0)
            conv(0)
            sum_rows(1)
            conv(1)
            logits(1)
            conv(2)
            spread(1)
            conv(3)
            aggregate(1)
            mean_through_kernels(1)
            for b in range(4, B):
                conv(b)


_OUT = (B, C, H, W)


def kernel(**inputs):
    import concourse.bacc as bacc
    from concourse.bass_utils import run_bass_kernel_spmd as run

    def array(name):
        return np.ascontiguousarray(np.asarray(inputs[name]))

    params = np.concatenate([array("L0_conv_fc_w").T, array("L1_conv_ksm_w").T, array("L0_conv_fc_b").reshape(C, 1),
                             array("L1_conv_bias").reshape(C, 1), array("L1_conv_fbm_scale").reshape(C, 1)], axis=1)
    arrays = {"x": array("x"), "w_modes": array("L0_conv_weight"), "dft_w": array("L1_conv_dft_weight"),
              "params": np.ascontiguousarray(params), "consts": constants()}
    nc = bacc.Bacc("TRN2", target_bir_lowering=False, num_devices=1)
    args = [nc.dram_tensor(n, a.shape, F32, kind="ExternalInput").ap() for n, a in arrays.items()]
    out = nc.dram_tensor("out", _OUT, F32, kind="ExternalOutput").ap()
    spectral_then_attention_conv(nc, *args, out)
    r = run(nc, [arrays], core_ids=[0])
    return r.results[0]["out"]
```

```python
from contextlib import ExitStack

import numpy as np
import concourse.bass as bass
from concourse import mybir

F32 = mybir.dt.float32
ALU = mybir.AluOpType
ACT = mybir.ActivationFunctionType
AX_X = mybir.AxisListType.X

B, C, H, W = 8, 32, 64, 64
M1 = 32
NPIX = H * W
EPS = 1e-5
K_NUM = 16
CLIP = 10.0
CHUNKS = [8, 8, 8, 4, 2, 2]
FIRST = [sum(CHUNKS[:k]) for k in range(len(CHUNKS))]
SLOTS = 3
WP = W + 2
UB = 16
SIN60 = float(np.sqrt(3.0) / 2)

CONSTS = ["fwd_h", "fwd_cos", "fwd_sin", "fwd_nsin", "inv_re", "inv_im", "inv_w", "mean_c", "eye", "spread"]
MASK4 = 128 * len(CONSTS)
HALF2 = MASK4 + 4
MASKK = HALF2 + 2
NCONST = MASKK + 4
TAP_N = 9 * 32 + 1
P_FC, P_KSM, P_FCB, P_BIAS, P_SCALE = 0, 32, 48, 49, 50
NPARAM = 51


def constants():
    th = 2 * np.pi / H
    m = np.arange(M1)
    h = np.arange(H) - (H - 1) / 2
    half = np.arange(W // 2) + 0.5
    out = np.zeros((128, NCONST), np.float64)

    def put(name, a):
        k = 128 * CONSTS.index(name)
        out[:, k:k + 128] = a.reshape(128, 128)

    a = np.zeros((2, H, 2, 2, 8, 4))
    for p in range(2):
        for mg in range(4):
            t = th * np.outer(h, 8 * mg + np.arange(8))
            a[p, :, p, 0, :, mg] = np.cos(t)
            a[p, :, p, 1, :, mg] = -np.sin(t)
    put("fwd_h", a)
    for name, f in (("fwd_cos", np.cos), ("fwd_sin", np.sin), ("fwd_nsin", lambda t: -np.sin(t))):
        a = np.zeros((4, W // 2, 4, M1))
        for q in range(4):
            a[q, :, q, :] = f(th * np.outer(half, m))
        put(name, a)
    for name, (fr, fi) in (("inv_re", (np.cos, lambda t: -np.sin(t))), ("inv_im", (np.sin, np.cos))):
        a = np.zeros((2, 8, 4, 2, 2, H))
        for x in range(2):
            for ml in range(8):
                for mg in range(4):
                    t = th * (8 * mg + ml) * h
                    a[x, ml, mg, 0, x] = fr(t)
                    a[x, ml, mg, 1, x] = fi(t)
        put(name, a)
    a = np.zeros((2, 2, M1, 2, W))
    weight = np.where(m == 0, 1.0, 2.0)[:, None] / NPIX
    for y in range(2):
        a[0, y, :, y] = weight * np.cos(th * np.outer(m, h))
        a[1, y, :, y] = -weight * np.sin(th * np.outer(m, h))
    put("inv_w", a)
    put("mean_c", np.tile(np.eye(32), (4, 4)) / NPIX)
    put("eye", np.tile(np.eye(32), (4, 4)))
    a = np.zeros((128, 4, 32))
    for k in range(K_NUM):
        a[k, k % 4] = 1
        out[k, MASKK + k // 4] = 1
    put("spread", a)
    for j in range(4):
        out[32 * j:32 * j + 32, MASK4 + j] = 1
    for p in range(2):
        out[64 * p:64 * p + 64, HALF2 + p] = 1
    return out.astype(np.float32)


def spectral_then_attention_conv(nc, x, w_modes, dft_w, params, scale, consts, out):
    with ExitStack() as ctx:
        def sb(name, n):
            return ctx.enter_context(nc.sbuf_tensor(name, [128, n], F32))

        def sem(name):
            return ctx.enter_context(nc.semaphore(name))

        cst = sb("cst", NCONST)
        prm = sb("prm", NPARAM)
        x_buf = sb("x_buf", 4 * C * W)
        fold_buf = sb("fold_buf", 8192)
        y_buf = sb("y_buf", B * UB * WP)
        w_buf = sb("w_buf", B * (UB + 1) * WP)
        bd_buf = sb("bd_buf", 4096)
        q_buf = sb("q_buf", 4096)
        sq_trash, att_diag, spread_att = q_buf[:, 0:2048], q_buf[:, 2048:2560], q_buf[:, 2560:3072]
        r_buf = sb("r_buf", 4096)
        taps = sb("taps", 4 * TAP_N)
        conv_w = [sb(f"conv_w{r}", B * 3 * 32) for r in range(2)]
        fc_diag = sb("fc_diag", 128)
        row_sq = sb("row_sq", 4 * 32)[:].rearrange("p (q c) -> p q c", q=4)
        stat1 = sb("stat1", 8 * 7)
        bconst = sb("bconst", 2)
        kern = sb("kern", 3 * 288 + 32)
        st2 = sb("st2", 160)

        def const(name):
            k = 128 * CONSTS.index(name)
            return cst[:, k:k + 128]

        mask4 = cst[:, MASK4:MASK4 + 4]
        ones2 = cst[:, HALF2:HALF2 + 2]
        eye32 = const("eye")[:, 0:32]

        xh = x_buf[:].rearrange("p (q c w) -> p q c w", q=4, c=C)
        xr = x_buf[:].rearrange("p (b u w) -> p b u w", b=B, u=UB)
        fold = fold_buf[:].rearrange("p (c e q w) -> p c e q w", c=C, e=2, q=4)
        t_rows = fold_buf[:].rearrange("p (g x h c) -> p g x h c", g=2, x=2, c=C)
        dft_sb = fold_buf[:, 0:2304]
        dft_v = fold_buf[:, 2304:4608].rearrange("p (r u v k) -> p r u v k", r=2, u=3, v=3)
        dft_t = fold_buf[:, 4608:4608 + 4 * 384].rearrange("p (t n) -> p t n", t=4)
        y_rows = y_buf[:, 0:8192].rearrange("p (e f c) -> p e f c", e=2, c=C)
        xa = y_buf[:].rearrange("p (b u w) -> p b u w", b=B, u=UB)
        xb = w_buf[:].rearrange("p (b u w) -> p b u w", b=B, u=UB + 1)
        modes = w_buf[:, 0:8192].rearrange("p (xo ml n) -> p xo ml n", xo=64, ml=4)
        bd = [t[:].rearrange("p (n x b g r) -> p n x b g r", n=M1, x=2, b=B, g=4) for t in (bd_buf, r_buf)]
        ost = bd_buf[:, 0:2048].rearrange("p (s n) -> p s n", s=2)

        def x_squares(k):
            at = 2048 * (k % 2)
            return q_buf[:, at:at + 4 * W * CHUNKS[k]].rearrange("p (q c w) -> p q c w", q=4, w=W)

        mixed = q_buf[:].rearrange("p (nl b ml g) -> p nl b ml g", nl=8, b=B, ml=8)
        r_modes = r_buf[:].rearrange("p (g o y n) -> p g o y n", g=2, y=2, o=32)
        tap_n = taps[:].rearrange("p (k n) -> p k n", k=4)
        tap = tap_n[:, :, 0:288].rearrange("p k (t i) -> p k t i", t=9)
        cw = [t[:].rearrange("p (b k o) -> p b k o", b=B, k=3) for t in conv_w]
        mean1, msq1, var1, std1, rstd1, dc1, tmp1 = (stat1[:, 8 * k:8 * k + 8] for k in range(7))

        part = st2[:, 0:32].rearrange("p (g s b h) -> p g s b h", g=2, s=2, b=4)
        avg = st2[:, 32:48].rearrange("p (g s b) -> p g s b", g=2, s=2)
        names = ["rowsum", "var", "std", "rstd", "pool", "mdiag", "rdiag", "btot", "t", "centred", "const"]
        g2 = {k: st2[:, 48 + 8 * i:56 + 8 * i].rearrange("p (g b) -> p g b", g=2) for i, k in enumerate(names)}
        rd1, rsum = st2[:, 136:137], st2[:, 137:138]
        soft = sb("soft", 2 * 32)
        scale_row = sb("scale_row", 32)
        scale_in = sb("scale_in", 32)
        slot = [ctx.enter_context(nc.psum_tensor(f"slot{i}", [128, 1024], F32)) for i in range(SLOTS)]
        small = ctx.enter_context(nc.psum_tensor("small", [128, 512], F32))
        aggp = ctx.enter_context(nc.psum_tensor("aggp", [128, 512], F32))

        fwd_h_in = sem("fwd_h_in"); cst_in = sem("cst_in"); prm_in = sem("prm_in")
        xh_in = [sem(f"xh_in{k}") for k in range(len(CHUNKS))]
        xh_pool_in = sem("xh_pool_in")
        scale_row_in = sem("scale_row_in")
        modes_in = sem("modes_in")
        xr_in = [sem(f"xr_in{k}") for k in range(4)]; dft_in = sem("dft_in"); stored = [sem(f"stored{k}") for k in range(2)]
        f1_done = sem("f1_done"); stat_done = sem("stat_done"); f2_done = sem("f2_done")
        mix_done = sem("mix_done"); fc_done = sem("fc_done"); i1_done = sem("i1_done")
        i2_done = sem("i2_done"); sum_done = sem("sum_done"); logits_done = sem("logits_done")
        spread_done = sem("spread_done"); agg_done = sem("agg_done")
        conv_done = sem("conv_done"); bias_done = sem("bias_done")
        sq_ready = sem("sq_ready"); y_ready = sem("y_ready"); std_ready = sem("std_ready")
        mixed_ready = sem("mixed_ready"); r_act = sem("r_act"); t_act = sem("t_act")
        sq2_ready = sem("sq2_ready"); std2_ready = sem("std2_ready"); exp_ready = sem("exp_ready")
        w1_ready = sem("w1_ready"); out_act = sem("out_act")
        fold_ready = sem("fold_ready"); sq_used = sem("sq_used");
        var_ready = sem("var_ready"); bd_ready = sem("bd_ready"); fcd_ready = sem("fcd_ready")
        r_dve = sem("r_dve"); t_dve = sem("t_dve"); xa_ready = sem("xa_ready"); out_dve = sem("out_dve")
        xb_in = [sem(f"xb_in{b}") for b in range(B)]
        kern_ready = sem("kern_ready")
        var2_ready = sem("var2_ready"); pool_ready = sem("pool_ready"); mdiag_ready = sem("mdiag_ready")
        sigmoid_ready = sem("sigmoid_ready"); num_ready = sem("num_ready"); ksum_ready = sem("ksum_ready")
        bias_ready = sem("bias_ready")
        mixed_dve = sem("mixed_dve")
        att_ready = sem("att_ready"); w0_ready = sem("w0_ready"); pads_ready = sem("pads_ready")
        dve = sem("dve_done")
        bd_zero = sem("bd_zero"); w_zero = sem("w_zero"); pool = sem("pool_done"); taps_ready = sem("taps_ready")

        users = [("f1", k) for k in range(8)] + [("f2", k) for k in range(3)]
        users += [("mix", k) for k in range(4)] + [("f2", 3)] + [("mix", k) for k in range(4, 8)]
        users += [("fc", k) for k in range(4)]
        users += [("i1", k) for k in range(5)] + [("i2", k) for k in range(4)]
        users += [("i1", k) for k in range(5, 8)] + [("i2", k) for k in range(4, 8)]
        users += [("conv", b) for b in range(B)]
        slot_of = {}
        for u in users:
            slot_of[u] = len(slot_of) % SLOTS
        slot_of.update({("mix", k): (slot_of["f2", 0], slot_of["f2", 1])[k % 2] for k in range(8)})
        slot_of["f2", 3] = slot_of["f2", 2]
        first = users.index(("fc", 0))
        slot_of.update({u: (slot_of["f2", 2] + n) % SLOTS for n, u in enumerate(users[first:])})
        freed = {"f1": lambda k: [(y_ready, k + 1)],
                 "f2": lambda k: [(bd_ready, 2 * (k + 1))],
                 "mix": lambda k: [(mixed_ready, (4, 8, 12, 16, 20, 24, 26, 30)[k])] + ([(mixed_dve, 2 + 4 * (k - 6))] if k >= 6 else []),
                 "fc": lambda k: [(r_act, 2 * (k + 1)), (r_dve, 2 * (k + 1))],
                 "i1": lambda k: [(t_act, k + 1), (t_dve, k + 1)],
                 "i2": lambda k: [(xa_ready, 2 * (k + 1))],
                 "conv": lambda k: [(out_act, k + 1), (out_dve, k + 1)]}

        def take_slot(pe, user):
            before = [u for u in users[:users.index(user)] if slot_of[u] == slot_of[user]]
            if before:
                stage, k = before[-1]
                for s, v in freed[stage](k):
                    pe.wait_ge(s, v)
            return slot[slot_of[user]]

        def mixed_part(k, t, xx, bank=None):
            ml, nh = divmod(k, 2)
            ps = slot[slot_of["mix", k]][:].rearrange("p (nl x b g) -> p nl x b g", nl=8, x=2, b=B)
            src, dst = 32 * (2 * t + xx), 32 * (2 * t + nh)
            nls = slice(0, 8) if bank is None else slice(4 * bank, 4 * bank + 4)
            return mixed[dst:dst + 32, nls, :, 4 * xx + ml, :], ps[src:src + 32, nls, xx]

        def turned(k, half, g):
            dst = r_modes[:, g].rearrange("p o y (nq nl) -> p y nq o nl", nq=4)[:, :, :, :, 2 * k + half]
            c0 = 512 * half + 256 * g
            return dst, slot[slot_of["fc", k]][:, c0:c0 + 256].rearrange("p (y q o) -> p y q o", y=2, q=4)

        def rows(k, half):
            g, c0 = k // 4, 8 * (k % 4) + 4 * half
            dst = t_rows[:, g, :, :, c0:c0 + 4].rearrange("p x h c -> p c x h")
            return dst, slot[slot_of["i1", k]][:, 512 * half:512 * half + 512].rearrange("p (c x h) -> p c x h", c=4, x=2)

        def load_rows(eng, k, b, landed):
            p, q = divmod(b, 4)
            cs = slice(FIRST[k], FIRST[k] + CHUNKS[k])
            eng.dma_start(xh[64 * p:64 * p + 64, q, cs, :], x[b, cs].rearrange("c h w -> h c w")).then_inc(landed, 16)

        def load_channel(eng, c, p, landed):
            eng.dma_start(xh[64 * p:64 * p + 64, :, c, :], x[4 * p:4 * p + 4, c].rearrange("q h w -> h q w")
                          ).then_inc(landed, 16)

        def rows_landed(eng, k):
            eng.wait_ge(xh_in[k], 16 * (B // 2 if k == 0 else B if CHUNKS[k] > 2 else 2 * CHUNKS[k]))
            if k == 0:
                eng.wait_ge(xh_pool_in, 16 * (B // 2))

        block = ctx.enter_context(nc.Block())

        @block.sync
        def _(sp):
            sp.dma_start(cst[:, 0:128], consts[:, 0:128]).then_inc(fwd_h_in, 16)
            for k, n in enumerate(CHUNKS):
                if n > 2:
                    for b in range(4 if k == 0 else 0, B):
                        load_rows(sp, k, b, xh_in[k])
                else:
                    for c in range(FIRST[k], FIRST[k] + n):
                        for p in range(2):
                            load_channel(sp, c, p, xh_in[k])
            sp.dma_start(cst[:, 128:NCONST], consts[:, 128:NCONST]).then_inc(cst_in, 16)
            for xx in range(2):
                for mg in range(4):
                    m0 = 8 * mg + 4 * xx
                    sp.dma_start(modes[32 * mg:32 * mg + 32, 32 * xx:32 * xx + 32].rearrange("i o m n -> i o (m n)"),
                                 w_modes[0, :, :, m0:m0 + 4, :].rearrange("i o m n -> i o (m n)")).then_inc(modes_in, 16)
            for j in range(4):
                sp.dma_start(prm[32 * j:32 * j + 32, :], params).then_inc(prm_in, 16)
            sp.dma_start(scale_row[:], scale.partition_broadcast(128)).then_inc(scale_row_in, 16)
            sp.wait_ge(f1_done, 8)
            sp.dma_start(dft_sb.rearrange("p (k n) -> p k n", k=4),
                         dft_w.rearrange("(kg kl) o i kh kw z -> (kl o) kg (i kh kw z)", kg=4)).then_inc(dft_in, 16)
            sp.wait_ge(fold_ready, 2 * len(CHUNKS))
            sp.wait_ge(sq_ready, len(CHUNKS))
            for b in (0, 2, 1, 3, 4, 6, 5, 7):
                for j in range(4):
                    sp.dma_start(xr[32 * j:32 * j + 32, b],
                                 x[b].rearrange("c (u j) w -> j c u w", j=4)[j]).then_inc(xr_in[2 * (b // 4) + b % 2], 16)
            for n, b in enumerate((0, 2, 1, 3, 4, 6, 5, 7)):
                sp.wait_ge(xa_ready, 4 * (n // 2 + 1))
                sp.dma_start(xb[0:64, b, 1:UB + 1, 1:W + 1], xa[64:128, b, :, 1:W + 1]).then_inc(xb_in[b], 16)
                sp.dma_start(xb[64:128, b, 0:UB, 1:W + 1], xa[0:64, b, :, 1:W + 1]).then_inc(xb_in[b], 16)
            for b in range(B):
                sp.wait_ge(out_act, b + 1)
                parts = 2 if b == B - 1 else 1
                for n in range(parts):
                    if n == parts - 1:
                        sp.wait_ge(out_dve, b + 1)
                    us = slice(UB // parts * n, UB // parts * (n + 1))
                    for j in range(4):
                        sp.dma_start(out[b].rearrange("c (u j) w -> j c u w", j=4)[j, :, us],
                                     ost[32 * j:32 * j + 32, b % 2].rearrange("c (u w) -> c u w", w=W)[:, us]
                                     ).then_inc(stored[b % 2], 16)
            sp.wait_ge(stored[0], 16 * 4 * (B // 2))
            sp.wait_ge(stored[1], 16 * 4 * (B // 2 + 1))

        @block.gpsimd
        def _(gp):
            for b in range(4):
                load_rows(gp, 0, b, xh_pool_in)
            nc.gpsimd.memset(bd_buf[:], 0.0).then_inc(bd_zero, 1)
            gp.wait_ge(bd_zero, 1)
            nc.gpsimd.memset(r_buf[:], 0.0).then_inc(bd_zero, 1)
            gp.wait_ge(bd_zero, 2)
            nc.gpsimd.memset(conv_w[0][96:128, :], 0.0).then_inc(w_zero, 1)
            gp.wait_ge(w_zero, 1)
            nc.gpsimd.memset(conv_w[1][0:32, :], 0.0).then_inc(w_zero, 1)

            gp.wait_ge(dft_in, 16)
            gp.wait_ge(w_zero, 2)
            a = dft_sb.rearrange("p (k u v z) -> p z v u k", u=3, v=3, z=2)
            steps = 0

            def step(ins):
                nonlocal steps
                steps += 1
                ins.then_inc(pool, 1)
                gp.wait_ge(pool, steps)

            def tt(o, p, q, op):
                step(nc.gpsimd.tensor_tensor(o, p, q, op))

            def scaled(o, p, f):
                step(nc.gpsimd.tensor_scalar(o, p, f, None, ALU.mult))

            def n3(t):
                return dft_t[:, t, :].rearrange("p (u k) -> p u k", u=3)

            for z in range(2):
                tt(n3(z), a[:, z, 1], a[:, z, 2], ALU.add)
                tt(n3(2 + z), a[:, z, 1], a[:, z, 2], ALU.subtract)
            for z in range(2):
                tt(dft_v[:, z, :, 0], a[:, z, 0], n3(z), ALU.add)
            for z in range(2):
                scaled(n3(z), n3(z), -0.5)
                scaled(n3(2 + z), n3(2 + z), SIN60)
            for z in range(2):
                tt(n3(z), n3(z), a[:, z, 0], ALU.add)
            for z, first, second in ((0, ALU.subtract, ALU.add), (1, ALU.add, ALU.subtract)):
                tt(dft_v[:, z, :, 1], n3(z), n3(3 - z), first)
                tt(dft_v[:, z, :, 2], n3(z), n3(3 - z), second)
            re, im = dft_v[:, 0], dft_v[:, 1]

            def row(kh):
                return tap[:, :, 3 * kh:3 * kh + 3, :].rearrange("p k t i -> p t k i")

            def by_kernel(t):
                return t.rearrange("p v (k i) -> p v k i", k=4)

            tt(n3(0), re[:, 1], re[:, 2], ALU.add)
            tt(n3(1), im[:, 1], im[:, 2], ALU.subtract)
            tt(row(0), by_kernel(re[:, 0]), by_kernel(n3(0)), ALU.add)
            scaled(n3(2), n3(0), -0.5)
            scaled(n3(1), n3(1), SIN60)
            tt(n3(3), n3(2), re[:, 0], ALU.add)
            tt(row(1), by_kernel(n3(3)), by_kernel(n3(1)), ALU.subtract)
            tt(row(2), by_kernel(n3(3)), by_kernel(n3(1)), ALU.add)
            nc.gpsimd.memset(tap_n[:, :, 288:289], 3.0).then_inc(taps_ready, 1)

        @block.scalar
        def _(act):
            def copy_y(k):
                act.wait_ge(f1_done, k + 1)
                act.activation(y_rows[:, :, :, 4 * k:4 * k + 4].rearrange("p e f c -> p c e f"),
                               slot[slot_of["f1", k]][:].rearrange("p (c e f) -> p c e f", c=4, e=2),
                               ACT.Copy).then_inc(y_ready, 1)

            copied = 0
            for k, n in enumerate(CHUNKS):
                rows_landed(act, k)
                if k >= 2:
                    act.wait_ge(sq_used, k - 1)
                act.activation(x_squares(k), xh[:, :, FIRST[k]:FIRST[k] + n, :], ACT.Square).then_inc(sq_ready, 1)
                while 4 * copied < (C if k == len(CHUNKS) - 1 else FIRST[k]):
                    copy_y(copied)
                    copied += 1
            act.wait_ge(var_ready, 1)
            act.activation(std1, var1, ACT.Sqrt).then_inc(std_ready, 1)
            for k in range(8):
                for bank in (None,) if k < 7 else (0, 1):
                    act.wait_ge(mix_done, k + 1 + (bank or 0))
                    for t in range(2 if k < 6 else 1):
                        for xx in range(2):
                            act.activation(*mixed_part(k, t, xx, bank), ACT.Copy).then_inc(mixed_ready, 1)
            for k in range(4):
                act.wait_ge(fc_done, 2 * k + 1)
                for g in range(2):
                    act.activation(*turned(k, 0, g), ACT.Copy).then_inc(r_act, 1)

            def copy_t(k):
                act.wait_ge(i1_done, 2 * k + 1)
                if k == 0:
                    act.wait_ge(taps_ready, 1)
                act.activation(*rows(k, 0), ACT.Copy).then_inc(t_act, 1)

            def squares(k, n):
                g, x, half = k // 4, (k // 2) % 2, k % 2
                act.wait_ge(xa_ready, 2 * k + 2)
                for y in range(2):
                    if n >= 1:
                        act.wait_ge(sq2_ready, 2 * n - 1 + y)
                    act.activation(sq_trash[:, 512 * y:512 * y + 512].rearrange("p (u w) -> p u w", u=8),
                                   xa[:, 4 * g + 2 * y + x, 8 * half:8 * half + 8, 1:W + 1], ACT.Square,
                                   accum_out=part[:, g, 1, 2 * y + x, half:half + 1]).then_inc(sq2_ready, 1)

            def finish_stats(g):
                act.wait_ge(var2_ready, g + 1)
                act.activation(g2["std"][:, g], g2["var"][:, g], ACT.Sqrt).then_inc(std2_ready, 1)

            def softmax(g):
                z = soft[0:K_NUM, 32 * g:32 * g + 32]
                act.wait_ge(logits_done, g + 1)
                act.activation(z[:, 0:4], small[0:K_NUM, 64:68], ACT.Exp, scale=-1.0 / NPIX).then_inc(exp_ready, 1)
                act.wait_ge(sigmoid_ready, g + 1)
                act.activation(z[:, 12:16], z[:, 8:12], ACT.Exp).then_inc(exp_ready, 1)

            def weights(g):
                act.wait_ge(kern_ready, g + 1)
                kt = kern[:, 576:864]
                for i in range(4):
                    for kh in range(3):
                        j = kh + 1
                        act.activation(conv_w[1][32 * j:32 * j + 32, 96 * (4 * g + i):96 * (4 * g + i) + 96],
                                       kt[32 * i:32 * i + 32, 96 * kh:96 * kh + 96], ACT.Copy).then_inc(w1_ready, 1)

            def out_copy(b):
                act.wait_ge(conv_done, 2 * b + 1)
                if b % 4 == 0:
                    act.wait_ge(bias_ready, b // 4 + 1)
                if b >= 2:
                    act.wait_ge(stored[b % 2], 64 * (b // 2))
                act.activation(ost[:, b % 2, 0:512], slot[slot_of["conv", b]][:, 0:512], ACT.Identity,
                               bias=g2["btot"][:, b // 4, b % 4:b % 4 + 1]).then_inc(out_act, 1)

            for k in range(5):
                copy_t(k)
            for k in range(4):
                squares(k, k)
            copy_t(5)
            copy_t(6)
            finish_stats(0)
            copy_t(7)
            softmax(0)
            squares(4, 4)
            weights(0)
            squares(5, 5)
            squares(6, 6)
            squares(7, 7)
            finish_stats(1)
            out_copy(0)
            softmax(1)
            out_copy(1)
            weights(1)
            for b in range(2, B):
                out_copy(b)

        @block.vector
        def _(v):
            done = 0

            def chain(ins):
                nonlocal done
                done += 1
                ins.then_inc(dve, 1)
                v.wait_ge(dve, done)

            def fold_x(k):
                cs = slice(FIRST[k], FIRST[k] + CHUNKS[k])
                rows_landed(v, k)
                right, left = xh[:, :, cs, 32:64], xh[:, :, cs, 31::-1]
                for e, op in ((0, ALU.add), (1, ALU.subtract)):
                    nc.vector.tensor_tensor(fold[:, cs, e].rearrange("p c q w -> p q c w"), right, left,
                                            op).then_inc(fold_ready, 1)

            def sum_squares(k, c0, c1):
                v.wait_ge(sq_ready, k + 1)
                ins = nc.vector.tensor_reduce(row_sq[:, :, FIRST[k] + c0:FIRST[k] + c1], x_squares(k)[:, :, c0:c1],
                                              AX_X, ALU.add)
                if c1 == CHUNKS[k]:
                    ins.then_inc(sq_used, 1)

            fold_x(0)
            sum_squares(0, 0, 8)
            fold_x(1)
            sum_squares(1, 0, 8)
            fold_x(2)
            sum_squares(2, 0, 4)
            fold_x(3)
            sum_squares(2, 4, 8)
            fold_x(4)
            fold_x(5)
            for k in range(3, len(CHUNKS)):
                sum_squares(k, 0, CHUNKS[k])

            v.wait_ge(stat_done, 1)
            nc.vector.tensor_scalar(mean1, small[:, 0:8], 1.0 / NPIX, None, ALU.mult)
            chain(nc.vector.tensor_scalar(msq1.rearrange("p (a b) -> p a b", a=2),
                                          small[:, 8:16].rearrange("p (q a) -> p a q", a=2), 1.0 / NPIX, EPS, ALU.mult, ALU.add))
            chain(nc.vector.tensor_tensor(tmp1, mean1, mean1, ALU.mult))
            nc.vector.tensor_tensor(var1, msq1, tmp1, ALU.subtract).then_inc(var_ready, 1)
            v.wait_ge(std_ready, 1)
            chain(nc.vector.reciprocal(rstd1, std1))
            chain(nc.vector.scalar_tensor_tensor(out=dc1, in0=mean1, scalar=float(NPIX), in1=rstd1, op0=ALU.mult, op1=ALU.mult))

            v.wait_ge(bd_zero, 2)
            for n in range(8):
                k, xx = divmod(n, 2)
                v.wait_ge(f2_done, n + 1)
                if k >= 2:
                    v.wait_ge(mix_done, 2 * (k - 1))
                z = slot[slot_of["f2", k]][:, 512 * xx:512 * xx + 512].rearrange("p (r b n) -> p r b n", r=2, b=B)
                for mg in range(4):
                    ps = slice(32 * mg, 32 * mg + 32)
                    ins = nc.vector.tensor_tensor(
                        bd[k % 2][ps, :, xx, :, mg, :].rearrange("p n b r -> p r b n"), z[ps],
                        rstd1[ps].unsqueeze(1).unsqueeze(3).broadcast_to([32, 2, B, M1]), ALU.mult)
                    if n == 0 and mg == 0:
                        chain(ins)
                        dc = bd[0][0:32, 0, 0, :, 0, 0]
                        chain(nc.vector.tensor_tensor(dc, dc, dc1[0:32], ALU.subtract))
                ins.then_inc(bd_ready, 1)

            v.wait_ge(prm_in, 64)
            v.wait_ge(cst_in, 16)
            nc.vector.tensor_tensor(fc_diag[:].rearrange("p (q o) -> p q o", q=4),
                                    prm[:, P_FC:P_FC + 32].unsqueeze(1).broadcast_to([128, 4, 32]),
                                    mask4.unsqueeze(2).broadcast_to([128, 4, 32]),
                                    ALU.mult).then_inc(fcd_ready, 1)
            chain(nc.vector.tensor_tensor(bconst[:, 0:1], prm[:, P_BIAS:P_BIAS + 1], prm[:, P_SCALE:P_SCALE + 1], ALU.mult))
            chain(nc.vector.tensor_tensor(bconst[:, 0:1], bconst[:, 0:1], prm[:, P_FCB:P_FCB + 1], ALU.add))

            for k, bank in ((6, None), (7, 0), (7, 1)):
                v.wait_ge(mix_done, k + 1 + (bank or 0))
                for xx in range(2):
                    nc.vector.tensor_copy(*mixed_part(k, 1, xx, bank)).then_inc(mixed_dve, 1)
            for k in range(4):
                v.wait_ge(fc_done, 2 * k + 2)
                for g in range(2):
                    nc.vector.tensor_copy(*turned(k, 1, g)).then_inc(r_dve, 1)

            def copy_t(k):
                v.wait_ge(i1_done, 2 * k + 2)
                if k == 0:
                    v.wait_ge(taps_ready, 1)
                nc.vector.tensor_copy(*rows(k, 1)).then_inc(t_dve, 1)

            def add_x(k):
                g, x, half = k // 4, (k // 2) % 2, k % 2
                v.wait_ge(i2_done, k + 1)
                ps = slot[slot_of["i2", k]][:].rearrange("p (u y w) -> p u y w", u=8, y=2)
                for y in range(2):
                    b = 4 * g + 2 * y + x
                    us = slice(8 * half, 8 * half + 8)
                    nc.vector.scalar_tensor_tensor(
                        out=xa[:, b, us, 1:W + 1], in0=ps[:, :, y, :], scalar=mean1[:, b:b + 1],
                        in1=xr[:, b, us, :], op0=ALU.subtract, op1=ALU.add,
                        accum_out=part[:, g, 0, 2 * y + x, half:half + 1]).then_inc(xa_ready, 1)

            def bcast(ap, *shape):
                whole = list(ap.shape) + list(shape)
                for _ in shape:
                    ap = ap.unsqueeze(len(ap.shape))
                return ap.broadcast_to(whole)

            def row_sums(g):
                v.wait_ge(xa_ready, 8 * (g + 1))
                chain(nc.vector.tensor_reduce(g2["rowsum"][:, g], part[:, g, 0], AX_X, ALU.add))

            def variance(g):
                mean, msq = avg[:, g, 0], avg[:, g, 1]
                v.wait_ge(sum_done, g + 1)
                chain(nc.vector.tensor_reduce(avg[:, g], small[:, 32:48].rearrange("p (s b h) -> p s b h", s=2, b=4),
                                              AX_X, ALU.add))
                chain(nc.vector.tensor_tensor(g2["t"][:, g], mean, mean, ALU.mult))
                nc.vector.scalar_tensor_tensor(out=g2["var"][:, g], in0=msq, scalar=EPS, in1=g2["t"][:, g],
                                               op0=ALU.add, op1=ALU.subtract).then_inc(var2_ready, 1)

            def pooled(g):
                chain(nc.vector.scalar_tensor_tensor(out=g2["centred"][:, g], in0=avg[:, g, 0], scalar=-float(NPIX // 4),
                                                     in1=g2["rowsum"][:, g], op0=ALU.mult, op1=ALU.add))
                v.wait_ge(std2_ready, g + 1)
                chain(nc.vector.reciprocal(g2["rstd"][:, g], g2["std"][:, g]))
                nc.vector.tensor_tensor(g2["pool"][:, g], g2["centred"][:, g], g2["rstd"][:, g], ALU.mult).then_inc(pool_ready, 1)

            def scales(g):
                nc.vector.tensor_tensor(g2["mdiag"][:, g], avg[:, g, 0], mask4, ALU.mult).then_inc(mdiag_ready, 1)
                chain(nc.vector.tensor_tensor(g2["rdiag"][:, g], g2["rstd"][:, g], mask4, ALU.mult))
                chain(nc.vector.tensor_reduce(rd1, g2["rdiag"][:, g], AX_X, ALU.add))
                chain(nc.vector.scalar_tensor_tensor(out=g2["const"][:, g], in0=mean1[:, 4 * g:4 * g + 4],
                                                     scalar=bconst[:, 0:1], in1=avg[:, g, 0], op0=ALU.add, op1=ALU.add))
                if g == 0:
                    v.wait_ge(scale_row_in, 16)
                chain(nc.vector.tensor_scalar(scale_in[:], scale_row[:], rd1, None, ALU.mult))

            def sigmoid(g):
                z = soft[0:K_NUM, 32 * g:32 * g + 32]
                v.wait_ge(exp_ready, 2 * g + 1)
                chain(nc.vector.tensor_scalar(z[:, 4:8], z[:, 0:4], 1.0, None, ALU.add))
                nc.vector.reciprocal(z[:, 8:12], z[:, 4:8]).then_inc(sigmoid_ready, 1)

            def by_group(g):
                z = soft[0:K_NUM, 32 * g:32 * g + 32]
                v.wait_ge(exp_ready, 2 * g + 2)
                nc.vector.tensor_tensor(z[:, 16:32].rearrange("p (k b) -> p k b", k=4),
                                        z[:, 12:16].unsqueeze(1).broadcast_to([K_NUM, 4, 4]),
                                        cst[0:K_NUM, MASKK:MASKK + 4].unsqueeze(2).broadcast_to([K_NUM, 4, 4]),
                                        ALU.mult).then_inc(num_ready, 1)

            def attention(g):
                v.wait_ge(spread_done, g + 1)
                nc.vector.tensor_tensor(
                    att_diag.rearrange("p (b k o) -> p b k o", b=4, k=4),
                    small[:, 128:144].rearrange("p (k b) -> p b k", k=4).unsqueeze(3).broadcast_to([128, 4, 4, 32]),
                    eye32.unsqueeze(1).unsqueeze(1).broadcast_to([128, 4, 4, 32]), ALU.mult).then_inc(att_ready, 1)

            def kernels(g):
                k0, k1, kt, ks = kern[:, 0:288], kern[:, 288:576], kern[:, 576:864], kern[:, 864:896]
                taps_of = kt.rearrange("p (t o) -> p t o", t=9)
                v.wait_ge(agg_done, g + 1)
                chain(nc.vector.reciprocal(rsum, aggp[:, 288:289]))
                chain(nc.vector.tensor_scalar(k0, aggp[:, 0:288], rsum, CLIP, ALU.mult, ALU.min))
                chain(nc.vector.transpose(k1, k0))
                if g:
                    v.wait_ge(w1_ready, 12 * g)
                chain(nc.vector.scalar_tensor_tensor(
                    out=taps_of, in0=k1.rearrange("p (t o) -> p t o", t=9), scalar=-CLIP,
                    in1=scale_in[:].unsqueeze(1).broadcast_to([128, 9, 32]), op0=ALU.max, op1=ALU.mult))
                nc.vector.tensor_tensor(kt[:, 128:160], kt[:, 128:160], eye32, ALU.add).then_inc(kern_ready, 1)
                v.wait_ge(kern_ready, g + 1)
                for i in range(4):
                    for kh in range(3):
                        at = 96 * (4 * g + i)
                        nc.vector.tensor_copy(conv_w[0][32 * kh:32 * kh + 32, at:at + 96],
                                              kt[32 * i:32 * i + 32, 96 * kh:96 * kh + 96]).then_inc(w0_ready, 1)
                nc.vector.tensor_reduce(ks, kt.rearrange("p (t o) -> p o t", t=9), AX_X, ALU.add).then_inc(ksum_ready, 1)

            def pads(g):
                bs = slice(4 * g, 4 * g + 4)
                mean = avg[:, g, 0]
                nc.vector.tensor_copy(xa[:, bs, :, 0:WP:WP - 1], bcast(mean, UB, 2))
                nc.vector.tensor_copy(xb[:, bs, :, 0:WP:WP - 1], bcast(mean, UB + 1, 2))
                nc.vector.tensor_copy(xb[0:64, bs, 0, 1:W + 1], bcast(mean[0:64], W))
                nc.vector.tensor_copy(xb[64:128, bs, UB, 1:W + 1], bcast(mean[64:128], W)).then_inc(pads_ready, 1)

            def bias_total(g):
                v.wait_ge(bias_done, g + 1)
                nc.vector.tensor_tensor(g2["btot"][:, g], g2["const"][:, g], small[:, 160:164],
                                        ALU.subtract).then_inc(bias_ready, 1)

            def out_copy(b):
                v.wait_ge(conv_done, 2 * b + 2)
                if b % 4 == 0:
                    v.wait_ge(bias_ready, b // 4 + 1)
                if b >= 2:
                    v.wait_ge(stored[b % 2], 64 * (b // 2))
                nc.vector.tensor_scalar(ost[:, b % 2, 512:1024], slot[slot_of["conv", b]][:, 512:1024],
                                        g2["btot"][:, b // 4, b % 4:b % 4 + 1], None, ALU.add).then_inc(out_dve, 1)

            for k in range(5):
                copy_t(k)
            for k in range(4):
                v.wait_ge(xr_in[k // 2], 128)
                add_x(k)
            row_sums(0)
            copy_t(5)
            copy_t(6)
            variance(0)
            pooled(0)
            copy_t(7)
            scales(0)
            pads(0)
            sigmoid(0)
            by_group(0)
            attention(0)
            v.wait_ge(xr_in[2], 128)
            add_x(4)
            add_x(5)
            kernels(0)
            v.wait_ge(xr_in[3], 128)
            add_x(6)
            add_x(7)
            row_sums(1)
            bias_total(0)
            variance(1)
            pooled(1)
            scales(1)
            pads(1)
            out_copy(0)
            sigmoid(1)
            by_group(1)
            attention(1)
            out_copy(1)
            kernels(1)
            out_copy(2)
            bias_total(1)
            for b in range(3, B):
                out_copy(b)

        @block.tensor
        def _(pe):
            def f1(k):
                ps = take_slot(pe, ("f1", k))
                for half in range(2):
                    c0 = 4 * k + 2 * half
                    chunk = max(i for i in range(len(CHUNKS)) if FIRST[i] <= c0)
                    for e in range(2):
                        pe.wait_ge(fold_ready, 2 * chunk + 1 + e)
                        for c in range(c0, c0 + 2):
                            col = 128 * (2 * (c - 4 * k) + e)
                            last = pe.matmul(ps[:, col:col + 128], fold[:, c, e].rearrange("p q w -> p (q w)"),
                                             const("fwd_h"), start=True, stop=True)
                last.then_inc(f1_done, 1)

            def f2(k):
                whole = slot[slot_of["f2", k]]
                if k < 3:
                    take_slot(pe, ("f2", k))
                for xx in range(2):
                    if k == 3:
                        pe.wait_ge(bd_ready, 5 + xx)
                    f2_half(whole[:, 512 * xx:512 * xx + 512], 4 * xx + k)

            def f2_half(ps, ml):

                def y(e, p, r):
                    f = 64 * p + 32 * r + 4 * ml
                    return y_rows[:, e, f:f + 4, :].rearrange("w g c -> w (g c)")

                for p in range(2):
                    re, im = ps[:, 128 * p:128 * p + 128], ps[:, 256 + 128 * p:384 + 128 * p]
                    pe.matmul(re, y(0, p, 0), const("fwd_cos"), start=True, stop=False)
                    pe.matmul(re, y(1, p, 1), const("fwd_sin"), start=False, stop=True)
                    pe.matmul(im, y(0, p, 1), const("fwd_cos"), start=True, stop=False)
                    last = pe.matmul(im, y(1, p, 0), const("fwd_nsin"), start=False, stop=True)
                last.then_inc(f2_done, 1)

            def mix(k):
                ps = take_slot(pe, ("mix", k))
                ml, nh = divmod(k, 2)
                if nh == 0:
                    pe.wait_ge(bd_ready, 2 * (ml + 1))
                if k == 0:
                    pe.wait_ge(modes_in, 16 * 8)
                for nl in range(8):
                    for t in range(2):
                        n = 16 * t + 8 * nh + nl
                        last = pe.matmul(ps[64 * t:64 * t + 64, 128 * nl:128 * nl + 128], modes[:, :, ml, n],
                                         bd[ml % 2][:, n].rearrange("p x b g r -> p (x b g r)"), start=True, stop=True)
                    if k == 7 and nl == 3:
                        last.then_inc(mix_done, 1)
                last.then_inc(mix_done, 1)

            def fc(k):
                ps = take_slot(pe, ("fc", k))
                for half in range(2):
                    for bb in range(4):
                        last = pe.matmul(ps[:, 512 * half + 128 * bb:512 * half + 128 * bb + 128],
                                         mixed[:, 2 * k + half, 2 * bb:2 * bb + 2].rearrange("p b m g -> p (b m g)"),
                                         fc_diag[:], start=True, stop=True)
                    last.then_inc(fc_done, 1)

            def i1(k):
                ps = take_slot(pe, ("i1", k))
                g, c0 = k // 4, 8 * (k % 4)
                for half in range(2):
                    for i in range(4):
                        for r, e in ((0, "inv_re"), (1, "inv_im")):
                            col = 512 * half + 128 * i
                            last = pe.matmul(ps[64 * r:64 * r + 64, col:col + 128], r_modes[:, g, c0 + 4 * half + i].rearrange("p y n -> p (y n)"),
                                             const(e), start=True, stop=True)
                    last.then_inc(i1_done, 1)

            def i2(k):
                ps = take_slot(pe, ("i2", k))
                g, x, u0 = k // 4, (k // 2) % 2, 8 * (k % 2)
                for u in range(8):
                    h = 4 * (u0 + u)
                    last = pe.matmul(ps[:, 128 * u:128 * u + 128],
                                     t_rows[:, g, x, h:h + 4, :].rearrange("p j c -> p (j c)"), const("inv_w"),
                                     start=True, stop=True)
                last.then_inc(i2_done, 1)

            def sum_rows(g):
                pe.wait_ge(xa_ready, 8 * (g + 1))
                pe.wait_ge(sq2_ready, 8 * (g + 1))
                if g:
                    pe.wait_ge(bias_ready, g)
                pe.matmul(small[:, 32:48], const("mean_c"), part[:, g].rearrange("p s b h -> p (s b h)"),
                          start=True, stop=True).then_inc(sum_done, 1)

            def logits(g):
                pe.wait_ge(pool_ready, g + 1)
                pe.matmul(small[0:K_NUM, 64:68], prm[:, P_KSM:P_KSM + K_NUM], g2["pool"][:, g], start=True,
                          stop=True).then_inc(logits_done, 1)

            def spread(g):
                pe.wait_ge(num_ready, g + 1)
                pe.matmul(small[:, 128:144], const("spread")[0:K_NUM], soft[0:K_NUM, 32 * g + 16:32 * g + 32],
                          start=True, stop=True).then_inc(spread_done, 1)

            def aggregate(g):
                pe.wait_ge(att_ready, g + 1)
                if g == 0:
                    pe.wait_ge(taps_ready, 1)
                for kg in range(4):
                    for i in range(4):
                        last = pe.matmul(aggp[32 * i:32 * i + 32, 0:TAP_N],
                                         att_diag[:, 128 * i + 32 * kg:128 * i + 32 * kg + 32],
                                         tap_n[:, kg], start=(kg == 0), stop=(kg == 3))
                last.then_inc(agg_done, 1)

            def mean_through_kernels(g):
                pe.wait_ge(ksum_ready, g + 1)
                pe.wait_ge(mdiag_ready, g + 1)
                for j in range(4):
                    last = pe.matmul(small[32 * j:32 * j + 32, 160:164], kern[:, 864:896], g2["mdiag"][:, g],
                                     start=True, stop=True)
                last.then_inc(bias_done, 1)

            def conv(b, half):
                if half == 0:
                    g = b // 4
                    if b % 4 == 0:
                        pe.wait_ge(w_zero, 2)
                        pe.wait_ge(pads_ready, g + 1)
                    pe.wait_ge(w0_ready, 3 * (b + 1))
                    pe.wait_ge(w1_ready, 3 * (b + 1))
                    pe.wait_ge(xb_in[b], 32)
                    take_slot(pe, ("conv", b))
                ps = slot[slot_of["conv", b]]
                u0 = 8 * half
                for kw in range(3):
                    for j, (r, src, u) in enumerate(((1, xb, u0), (0, xa, u0), (1, xa, u0), (0, xb, u0 + 1))):
                        last = pe.matmul(ps[32 * j:32 * j + 32, 512 * half:512 * half + 512], cw[r][:, b, kw, :],
                                         src[:, b, u:u + 8, kw:kw + W], start=(kw == 0), stop=(kw == 2))
                last.then_inc(conv_done, 1)

            pe.wait_ge(fwd_h_in, 16)
            for k in range(8):
                f1(k)
            pe.wait_ge(cst_in, 16)
            pe.wait_ge(sq_used, len(CHUNKS))
            for q in range(4):
                for mg in range(4):
                    pe.matmul(small[32 * mg:32 * mg + 32, 8 + 2 * q:10 + 2 * q], row_sq[:, q, :], ones2,
                              start=True, stop=True)
            pe.wait_ge(y_ready, 8)
            for p in range(2):
                for mg in range(4):
                    last = pe.matmul(small[32 * mg:32 * mg + 32, 4 * p:4 * p + 4], y_rows[:, 0, 64 * p, :], mask4,
                                     start=True, stop=True)
            last.then_inc(stat_done, 1)
            f2(0)
            f2(1)
            f2(2)
            for k in range(4):
                mix(k)
            f2(3)
            for k in range(4, 8):
                mix(k)
            pe.wait_ge(fcd_ready, 1)
            for k in range(4):
                if k % 2 == 0:
                    pe.wait_ge(mixed_ready, 28 + k)
                    pe.wait_ge(mixed_dve, 4 + k)
                fc(k)
            pe.wait_ge(r_act, 7)
            pe.wait_ge(r_dve, 7)
            for k in range(4):
                i1(k)
            i1(4)
            pe.wait_ge(t_act, 4)
            pe.wait_ge(t_dve, 4)
            for k in range(4):
                i2(k)
            i1(5)
            i1(6)
            sum_rows(0)
            i1(7)
            logits(0)
            pe.wait_ge(t_act, 8)
            pe.wait_ge(t_dve, 8)
            i2(4)
            spread(0)
            i2(5)
            aggregate(0)
            i2(6)
            i2(7)
            conv(0, 0)
            mean_through_kernels(0)
            conv(0, 1)
            sum_rows(1)
            conv(1, 0)
            logits(1)
            conv(1, 1)
            spread(1)
            conv(2, 0)
            aggregate(1)
            conv(2, 1)
            conv(3, 0)
            mean_through_kernels(1)
            conv(3, 1)
            for b in range(4, B):
                conv(b, 0)
                conv(b, 1)


_OUT = (B, C, H, W)


def kernel(**inputs):
    import concourse.bacc as bacc
    from concourse.bass_utils import run_bass_kernel_spmd as run

    def array(name):
        return np.ascontiguousarray(np.asarray(inputs[name]))

    params = np.concatenate([array("L0_conv_fc_w").T, array("L1_conv_ksm_w").T, array("L0_conv_fc_b").reshape(C, 1),
                             array("L1_conv_bias").reshape(C, 1), array("L1_conv_fbm_scale").reshape(C, 1)], axis=1)
    arrays = {"x": array("x"), "w_modes": array("L0_conv_weight"), "dft_w": array("L1_conv_dft_weight"),
              "params": np.ascontiguousarray(params), "scale": array("L1_conv_fbm_scale").reshape(C), "consts": constants()}
    nc = bacc.Bacc("TRN2", target_bir_lowering=False, num_devices=1)
    args = [nc.dram_tensor(n, a.shape, F32, kind="ExternalInput").ap() for n, a in arrays.items()]
    out = nc.dram_tensor("out", _OUT, F32, kind="ExternalOutput").ap()
    spectral_then_attention_conv(nc, *args, out)
    r = run(nc, [arrays], core_ids=[0])
    return r.results[0]["out"]
```

```python
from contextlib import ExitStack

import numpy as np
import concourse.bass as bass
from concourse import mybir

F32 = mybir.dt.float32
ALU = mybir.AluOpType
ACT = mybir.ActivationFunctionType
AX_X = mybir.AxisListType.X

B, C, H, W = 8, 32, 64, 64
M1 = 32
NPIX = H * W
EPS = 1e-5
K_NUM = 16
CLIP = 10.0
CHUNKS = [8, 8, 8, 4, 2, 2]
FIRST = [sum(CHUNKS[:k]) for k in range(len(CHUNKS))]
SLOTS = 3
WP = W + 2
UB = 16
SIN60 = float(np.sqrt(3.0) / 2)

CONSTS = ["fwd_h", "fwd_w_re", "fwd_w_im", "inv_re", "inv_im", "inv_w", "mean_c", "eye", "spread"]
MASK4 = 128 * len(CONSTS)
HALF2 = MASK4 + 4
MASKK = HALF2 + 2
NCONST = MASKK + 4
TAP_N = 9 * 32 + 1
DFT_READ = 12
P_FC, P_KSM, P_FCB, P_BIAS, P_SCALE = 0, 32, 48, 49, 50
NPARAM = 51


def constants():
    th = 2 * np.pi / H
    m = np.arange(M1)
    h = np.arange(H)
    out = np.zeros((128, NCONST), np.float64)

    def put(name, a):
        k = 128 * CONSTS.index(name)
        out[:, k:k + 128] = a.reshape(128, 128)

    a = np.zeros((2, H, 2, 2, 8, 4))
    for p in range(2):
        for mg in range(4):
            t = th * np.outer(h, 8 * mg + np.arange(8))
            a[p, :, p, 0, :, mg] = np.cos(t)
            a[p, :, p, 1, :, mg] = -np.sin(t)
    put("fwd_h", a)
    t = th * np.outer(h, m)
    for name, fr, fi in (("fwd_w_re", np.cos(t), -np.sin(t)), ("fwd_w_im", np.sin(t), np.cos(t))):
        a = np.zeros((2, W, 2, 2, M1))
        for q in range(2):
            a[q, :, q, 0] = fr
            a[q, :, q, 1] = fi
        put(name, a)
    for name, (fr, fi) in (("inv_re", (np.cos, lambda t: -np.sin(t))), ("inv_im", (np.sin, np.cos))):
        a = np.zeros((2, 8, 4, 2, 2, H))
        for x in range(2):
            for ml in range(8):
                for mg in range(4):
                    t = th * (8 * mg + ml) * h
                    a[x, ml, mg, 0, x] = fr(t)
                    a[x, ml, mg, 1, x] = fi(t)
        put(name, a)
    a = np.zeros((2, 2, M1, 2, W))
    weight = np.where(m == 0, 1.0, 2.0)[:, None] / NPIX
    for y in range(2):
        a[0, y, :, y] = weight * np.cos(th * np.outer(m, h))
        a[1, y, :, y] = -weight * np.sin(th * np.outer(m, h))
    put("inv_w", a)
    put("mean_c", np.tile(np.eye(32), (4, 4)) / NPIX)
    put("eye", np.tile(np.eye(32), (4, 4)))
    a = np.zeros((128, 4, 32))
    for k in range(K_NUM):
        a[k, k % 4] = 1
        out[k, MASKK + k // 4] = 1
    put("spread", a)
    for j in range(4):
        out[32 * j:32 * j + 32, MASK4 + j] = 1
    for p in range(2):
        out[64 * p:64 * p + 64, HALF2 + p] = 1
    return out.astype(np.float32)


def spectral_then_attention_conv(nc, x, w_modes, dft_w, params, scale, consts, out):
    with ExitStack() as ctx:
        def sb(name, n):
            return ctx.enter_context(nc.sbuf_tensor(name, [128, n], F32))

        def sem(name):
            return ctx.enter_context(nc.semaphore(name))

        cst = sb("cst", NCONST)
        prm = sb("prm", NPARAM)
        x_buf = sb("x_buf", 4 * C * W)
        t_buf = sb("t_buf", 8192)
        y_buf = sb("y_buf", B * UB * WP)
        w_buf = sb("w_buf", B * (UB + 1) * WP)
        bd_buf = sb("bd_buf", 4096)
        q_buf = sb("q_buf", 4096)
        sq_trash, att_diag = q_buf[:, 0:2048], q_buf[:, 2048:2560]
        r_buf = sb("r_buf", 4096)
        taps = sb("taps", 4 * TAP_N)
        conv_w = [sb(f"conv_w{r}", B * 3 * 32) for r in range(2)]
        fc_diag = sb("fc_diag", 128)
        row_sq = sb("row_sq", 4 * 32)[:].rearrange("p (q c) -> p q c", q=4)
        stat1 = sb("stat1", 8 * 7)
        bconst = sb("bconst", 2)
        kern = sb("kern", 3 * 288 + 32)
        st2 = sb("st2", 160)

        def const(name):
            k = 128 * CONSTS.index(name)
            return cst[:, k:k + 128]

        mask4 = cst[:, MASK4:MASK4 + 4]
        ones2 = cst[:, HALF2:HALF2 + 2]
        eye32 = const("eye")[:, 0:32]

        xh = x_buf[:].rearrange("p (c q w) -> p c q w", c=C, q=4)
        xr = x_buf[:].rearrange("p (b u w) -> p b u w", b=B, u=UB)
        t_rows = t_buf[:].rearrange("p (g x h c) -> p g x h c", g=2, x=2, c=C)
        dft_sb = t_buf[:, 0:2304]
        dft_v = t_buf[:, 4096:6400].rearrange("p (r u v k) -> p r u v k", r=2, u=3, v=3)
        dft_t = t_buf[:, 6400:6400 + 4 * 384].rearrange("p (t n) -> p t n", t=4)
        y_rows = y_buf[:, 0:8192].rearrange("p (s f c) -> p s f c", s=2, c=C)
        xa = y_buf[:].rearrange("p (b u w) -> p b u w", b=B, u=UB)
        xb = w_buf[:].rearrange("p (b u w) -> p b u w", b=B, u=UB + 1)
        modes = w_buf[:, 0:8192].rearrange("p (xo ml n) -> p xo ml n", xo=64, ml=4)
        bd = [t[:].rearrange("p (n x b g r) -> p n x b g r", n=M1, x=2, b=B, g=4) for t in (bd_buf, r_buf)]
        ost = bd_buf[:, 0:2048].rearrange("p (s n) -> p s n", s=2)

        def x_squares(k):
            at = 2048 * (k % 2)
            return q_buf[:, at:at + 4 * W * CHUNKS[k]].rearrange("p (c q w) -> p c q w", q=4, w=W)

        mixed = q_buf[:].rearrange("p (nl b ml g) -> p nl b ml g", nl=8, b=B, ml=8)
        r_modes = r_buf[:].rearrange("p (g o y n) -> p g o y n", g=2, y=2, o=32)
        tap_n = taps[:].rearrange("p (k n) -> p k n", k=4)
        tap = tap_n[:, :, 0:288].rearrange("p k (t i) -> p k t i", t=9)
        cw = [t[:].rearrange("p (b k o) -> p b k o", b=B, k=3) for t in conv_w]
        mean1, msq1, var1, std1, rstd1, dc1, tmp1 = (stat1[:, 8 * k:8 * k + 8] for k in range(7))

        part = st2[:, 0:32].rearrange("p (g s b h) -> p g s b h", g=2, s=2, b=4)
        avg = st2[:, 32:48].rearrange("p (g s b) -> p g s b", g=2, s=2)
        names = ["rowsum", "var", "std", "rstd", "pool", "mdiag", "rdiag", "btot", "t", "centred", "const"]
        g2 = {k: st2[:, 48 + 8 * i:56 + 8 * i].rearrange("p (g b) -> p g b", g=2) for i, k in enumerate(names)}
        rd1, rsum = st2[:, 136:137], st2[:, 137:138]
        soft = sb("soft", 2 * 32)
        scale_row = sb("scale_row", 32)
        scale_in = sb("scale_in", 32)
        slot = [ctx.enter_context(nc.psum_tensor(f"slot{i}", [128, 1024], F32)) for i in range(SLOTS)]
        small = ctx.enter_context(nc.psum_tensor("small", [128, 512], F32))
        aggp = ctx.enter_context(nc.psum_tensor("aggp", [128, 512], F32))

        fwd_h_in = sem("fwd_h_in"); cst_in = sem("cst_in"); prm_in = sem("prm_in")
        xh_in = [sem(f"xh_in{k}") for k in range(len(CHUNKS))]
        xh_pool_in = sem("xh_pool_in")
        scale_row_in = sem("scale_row_in")
        modes_in = sem("modes_in")
        xr_in = [sem(f"xr_in{k}") for k in range(4)]
        dft_in = sem("dft_in")
        xb_in = [sem(f"xb_in{b}") for b in range(B)]
        stored = [sem(f"stored{k}") for k in range(2)]
        f1_done = sem("f1_done"); stat_done = sem("stat_done"); f2_done = sem("f2_done")
        mix_done = sem("mix_done"); fc_done = sem("fc_done"); i1_done = sem("i1_done")
        i2_done = sem("i2_done"); sum_done = sem("sum_done"); logits_done = sem("logits_done")
        spread_done = sem("spread_done"); agg_done = sem("agg_done")
        conv_done = sem("conv_done"); bias_done = sem("bias_done")
        sq_ready = sem("sq_ready"); y_act = sem("y_act"); std_ready = sem("std_ready")
        mixed_ready = sem("mixed_ready"); r_act = sem("r_act"); t_act = sem("t_act")
        sq2_ready = sem("sq2_ready"); std2_ready = sem("std2_ready"); exp_ready = sem("exp_ready")
        w1_ready = sem("w1_ready"); out_act = sem("out_act")
        y_dve = sem("y_dve"); sq_used = sem("sq_used"); mixed_dve = sem("mixed_dve")
        var_ready = sem("var_ready"); bd_ready = sem("bd_ready"); fcd_ready = sem("fcd_ready")
        r_dve = sem("r_dve"); t_dve = sem("t_dve"); xa_ready = sem("xa_ready"); out_dve = sem("out_dve")
        kern_ready = sem("kern_ready")
        var2_ready = sem("var2_ready"); pool_ready = sem("pool_ready"); mdiag_ready = sem("mdiag_ready")
        sigmoid_ready = sem("sigmoid_ready"); num_ready = sem("num_ready"); ksum_ready = sem("ksum_ready")
        bias_ready = sem("bias_ready")
        att_ready = sem("att_ready"); w0_ready = sem("w0_ready"); pads_ready = sem("pads_ready")
        dve = sem("dve_done")
        bd_zero = sem("bd_zero"); w_zero = sem("w_zero"); pool = sem("pool_done"); taps_ready = sem("taps_ready")

        users = [("f1", k) for k in range(8)] + [("f2", k) for k in range(3)]
        users += [("mix", k) for k in range(4)] + [("f2", 3)] + [("mix", k) for k in range(4, 8)]
        users += [("fc", k) for k in range(4)]
        users += [("i1", k) for k in range(5)] + [("i2", k) for k in range(4)]
        users += [("i1", k) for k in range(5, 8)] + [("i2", k) for k in range(4, 8)]
        users += [("conv", b) for b in range(B)]
        slot_of = {}
        for u in users:
            slot_of[u] = len(slot_of) % SLOTS
        slot_of.update({("mix", k): (slot_of["f2", 0], slot_of["f2", 1])[k % 2] for k in range(8)})
        slot_of["f2", 3] = slot_of["f2", 2]
        first = users.index(("fc", 0))
        slot_of.update({u: (slot_of["f2", 2] + n) % SLOTS for n, u in enumerate(users[first:])})
        freed = {"f1": lambda k: [(y_act, k + 1), (y_dve, k + 1)] if k < 7 else [(y_act, 9)],
                 "f2": lambda k: [(bd_ready, 2 * (k + 1))],
                 "mix": lambda k: ([(mixed_ready, 4 * (k + 1))] if k < 6 else
                                   [(mixed_ready, 26), (mixed_dve, 2)] if k == 6 else
                                   [(mixed_ready, 30), (mixed_dve, 6)]),
                 "fc": lambda k: [(r_act, 2 * (k + 1)), (r_dve, 2 * (k + 1))],
                 "i1": lambda k: [(t_act, 2 * (k + 1) + 2 * (k == 7)), (t_dve, 2 * (k + 1) + 2 * (k == 7))],
                 "i2": lambda k: [(xa_ready, 2 * (k + 1))],
                 "conv": lambda k: [(out_act, k + 1), (out_dve, k + 1)]}

        def take_slot(pe, user):
            before = [u for u in users[:users.index(user)] if slot_of[u] == slot_of[user]]
            if before:
                stage, k = before[-1]
                for s, v in freed[stage](k):
                    pe.wait_ge(s, v)
            return slot[slot_of[user]]

        def mixed_part(k, t, xx, bank=None):
            ml, nh = divmod(k, 2)
            ps = slot[slot_of["mix", k]][:].rearrange("p (nl x b g) -> p nl x b g", nl=8, x=2, b=B)
            src, dst = 32 * (2 * t + xx), 32 * (2 * t + nh)
            nls = slice(0, 8) if bank is None else slice(4 * bank, 4 * bank + 4)
            return mixed[dst:dst + 32, nls, :, 4 * xx + ml, :], ps[src:src + 32, nls, xx]

        def turned(k, half, g):
            dst = r_modes[:, g].rearrange("p o y (nq nl) -> p y nq o nl", nq=4)[:, :, :, :, 2 * k + half]
            c0 = 512 * half + 256 * g
            return dst, slot[slot_of["fc", k]][:, c0:c0 + 256].rearrange("p (y q o) -> p y q o", y=2, q=4)

        def rows(k, odd, ri, bank=None):
            g, c0 = k // 4, 8 * (k % 4) + odd
            dst = t_rows[64 * ri:64 * ri + 64, g, :, :, c0:c0 + 7:2].rearrange("p x h c -> p c (x h)")
            src = slot[slot_of["i1", k]][64 * odd:64 * odd + 64, :].rearrange("p (c r h) -> p c r h", c=4, r=2)
            cs = slice(0, 4) if bank is None else slice(2 * bank, 2 * bank + 2)
            return dst[:, cs], src[:, cs, ri, :]

        def y_part(k, half):
            c0 = 4 * k + 2 * half
            return (y_rows[:, :, :, c0:c0 + 2].rearrange("p s f c -> p c s f"),
                    slot[slot_of["f1", k]][:, 512 * half:512 * half + 512].rearrange("p (c s f) -> p c s f", c=2, s=2))

        def load_rows(eng, k, b, landed):
            p, q = divmod(b, 4)
            cs = slice(FIRST[k], FIRST[k] + CHUNKS[k])
            eng.dma_start(xh[64 * p:64 * p + 64, cs, q, :], x[b, cs].rearrange("c h w -> h c w")).then_inc(landed, 16)

        def load_channel(eng, c, p, landed):
            eng.dma_start(xh[64 * p:64 * p + 64, c], x[4 * p:4 * p + 4, c].rearrange("q h w -> h q w")
                          ).then_inc(landed, 16)

        def rows_landed(eng, k):
            eng.wait_ge(xh_in[k], 16 * (B // 2 if k == 0 else B if CHUNKS[k] > 2 else 2 * CHUNKS[k]))
            if k == 0:
                eng.wait_ge(xh_pool_in, 16 * (B // 2))

        block = ctx.enter_context(nc.Block())

        @block.sync
        def _(sp):
            sp.dma_start(cst[:, 0:128], consts[:, 0:128]).then_inc(fwd_h_in, 16)
            for k, n in enumerate(CHUNKS):
                if n > 2:
                    for b in range(4 if k == 0 else 0, B):
                        load_rows(sp, k, b, xh_in[k])
                else:
                    for c in range(FIRST[k], FIRST[k] + n):
                        for p in range(2):
                            load_channel(sp, c, p, xh_in[k])
            sp.dma_start(cst[:, 128:NCONST], consts[:, 128:NCONST]).then_inc(cst_in, 16)
            for xx in range(2):
                for mg in range(4):
                    m0 = 8 * mg + 4 * xx
                    sp.dma_start(modes[32 * mg:32 * mg + 32, 32 * xx:32 * xx + 32].rearrange("i o m n -> i o (m n)"),
                                 w_modes[0, :, :, m0:m0 + 4, :].rearrange("i o m n -> i o (m n)")).then_inc(modes_in, 16)
            for j in range(4):
                sp.dma_start(prm[32 * j:32 * j + 32, :], params).then_inc(prm_in, 16)
            sp.dma_start(scale_row[:], scale.partition_broadcast(128)).then_inc(scale_row_in, 16)
            sp.dma_start(dft_sb.rearrange("p (k n) -> p k n", k=4),
                         dft_w.rearrange("(kg kl) o i kh kw z -> (kl o) kg (i kh kw z)", kg=4)).then_inc(dft_in, 16)
            sp.wait_ge(f1_done, 16)
            sp.wait_ge(sq_ready, len(CHUNKS))
            for b in (0, 2, 1, 3, 4, 6, 5, 7):
                for j in range(4):
                    sp.dma_start(xr[32 * j:32 * j + 32, b],
                                 x[b].rearrange("c (u j) w -> j c u w", j=4)[j]).then_inc(xr_in[2 * (b // 4) + b % 2], 16)
            for n, b in enumerate((0, 2, 1, 3, 4, 6, 5, 7)):
                sp.wait_ge(xa_ready, 4 * (n // 2 + 1))
                sp.dma_start(xb[0:64, b, 1:UB + 1, 1:W + 1], xa[64:128, b, :, 1:W + 1]).then_inc(xb_in[b], 16)
                sp.dma_start(xb[64:128, b, 0:UB, 1:W + 1], xa[0:64, b, :, 1:W + 1]).then_inc(xb_in[b], 16)
            for b in range(B):
                sp.wait_ge(out_act, b + 1)
                parts = 2 if b == B - 1 else 1
                for n in range(parts):
                    if n == parts - 1:
                        sp.wait_ge(out_dve, b + 1)
                    us = slice(UB // parts * n, UB // parts * (n + 1))
                    for j in range(4):
                        sp.dma_start(out[b].rearrange("c (u j) w -> j c u w", j=4)[j, :, us],
                                     ost[32 * j:32 * j + 32, b % 2].rearrange("c (u w) -> c u w", w=W)[:, us]
                                     ).then_inc(stored[b % 2], 16)
            sp.wait_ge(stored[0], 16 * 4 * (B // 2))
            sp.wait_ge(stored[1], 16 * 4 * (B // 2 + 1))

        @block.gpsimd
        def _(gp):
            for b in range(4):
                load_rows(gp, 0, b, xh_pool_in)
            nc.gpsimd.memset(bd_buf[:], 0.0).then_inc(bd_zero, 1)
            gp.wait_ge(bd_zero, 1)
            nc.gpsimd.memset(r_buf[:], 0.0).then_inc(bd_zero, 1)
            gp.wait_ge(bd_zero, 2)
            nc.gpsimd.memset(conv_w[0][96:128, :], 0.0).then_inc(w_zero, 1)
            gp.wait_ge(w_zero, 1)
            nc.gpsimd.memset(conv_w[1][0:32, :], 0.0).then_inc(w_zero, 1)

            gp.wait_ge(dft_in, 16)
            gp.wait_ge(w_zero, 2)
            a = dft_sb.rearrange("p (k u v z) -> p z v u k", u=3, v=3, z=2)
            steps = 0

            def step(ins):
                nonlocal steps
                steps += 1
                ins.then_inc(pool, 1)
                gp.wait_ge(pool, steps)

            def tt(o, p, q, op):
                step(nc.gpsimd.tensor_tensor(o, p, q, op))

            def scaled(o, p, f):
                step(nc.gpsimd.tensor_scalar(o, p, f, None, ALU.mult))

            def n3(t):
                return dft_t[:, t, :].rearrange("p (u k) -> p u k", u=3)

            for z in range(2):
                tt(n3(z), a[:, z, 1], a[:, z, 2], ALU.add)
                tt(n3(2 + z), a[:, z, 1], a[:, z, 2], ALU.subtract)
            for z in range(2):
                tt(dft_v[:, z, :, 0], a[:, z, 0], n3(z), ALU.add)
            for z in range(2):
                scaled(n3(z), n3(z), -0.5)
                scaled(n3(2 + z), n3(2 + z), SIN60)
            for z in range(2):
                tt(n3(z), n3(z), a[:, z, 0], ALU.add)
            assert steps == DFT_READ
            for z, first, second in ((0, ALU.subtract, ALU.add), (1, ALU.add, ALU.subtract)):
                tt(dft_v[:, z, :, 1], n3(z), n3(3 - z), first)
                tt(dft_v[:, z, :, 2], n3(z), n3(3 - z), second)
            re, im = dft_v[:, 0], dft_v[:, 1]

            def row(kh):
                return tap[:, :, 3 * kh:3 * kh + 3, :].rearrange("p k t i -> p t k i")

            def by_kernel(t):
                return t.rearrange("p v (k i) -> p v k i", k=4)

            tt(n3(0), re[:, 1], re[:, 2], ALU.add)
            tt(n3(1), im[:, 1], im[:, 2], ALU.subtract)
            tt(row(0), by_kernel(re[:, 0]), by_kernel(n3(0)), ALU.add)
            scaled(n3(2), n3(0), -0.5)
            scaled(n3(1), n3(1), SIN60)
            tt(n3(3), n3(2), re[:, 0], ALU.add)
            tt(row(1), by_kernel(n3(3)), by_kernel(n3(1)), ALU.subtract)
            tt(row(2), by_kernel(n3(3)), by_kernel(n3(1)), ALU.add)
            nc.gpsimd.memset(tap_n[:, :, 288:289], 3.0).then_inc(taps_ready, 1)

        @block.scalar
        def _(act):
            def copy_y(k):
                act.wait_ge(f1_done, 2 * k + 1)
                act.activation(*y_part(k, 0), ACT.Copy).then_inc(y_act, 1)

            copied = 0
            for k, n in enumerate(CHUNKS):
                rows_landed(act, k)
                if k >= 2:
                    act.wait_ge(sq_used, k - 1)
                act.activation(x_squares(k), xh[:, FIRST[k]:FIRST[k] + n], ACT.Square).then_inc(sq_ready, 1)
                while 4 * copied + 2 <= FIRST[k] + n:
                    copy_y(copied)
                    copied += 1
            act.wait_ge(f1_done, 16)
            act.activation(*y_part(7, 1), ACT.Copy).then_inc(y_act, 1)
            act.wait_ge(var_ready, 1)
            act.activation(std1, var1, ACT.Sqrt).then_inc(std_ready, 1)
            for k in range(8):
                for bank in (None,) if k < 7 else (0, 1):
                    act.wait_ge(mix_done, k + 1 + (bank or 0))
                    for t in range(2 if k < 6 else 1):
                        for xx in range(2):
                            act.activation(*mixed_part(k, t, xx, bank), ACT.Copy).then_inc(mixed_ready, 1)
            for k in range(4):
                act.wait_ge(fc_done, 2 * k + 1)
                for g in range(2):
                    act.activation(*turned(k, 0, g), ACT.Copy).then_inc(r_act, 1)

            def copy_t(k):
                act.wait_ge(i1_done, k + 1)
                if k == 0:
                    act.wait_ge(pool, DFT_READ)
                if k == 4:
                    act.wait_ge(taps_ready, 1)
                for ri in range(2):
                    act.activation(*rows(k, 0, ri), ACT.Copy).then_inc(t_act, 1)

            def copy_last_t(bank):
                act.wait_ge(i1_done, 8 + bank)
                for ri in range(2):
                    act.activation(*rows(7, 0, ri, bank), ACT.Copy).then_inc(t_act, 1)

            def squares(k, n):
                g, x, half = k // 4, (k // 2) % 2, k % 2
                act.wait_ge(xa_ready, 2 * k + 2)
                for y in range(2):
                    if n >= 1:
                        act.wait_ge(sq2_ready, 2 * n - 1 + y)
                    act.activation(sq_trash[:, 512 * y:512 * y + 512].rearrange("p (u w) -> p u w", u=8),
                                   xa[:, 4 * g + 2 * y + x, 8 * half:8 * half + 8, 1:W + 1], ACT.Square,
                                   accum_out=part[:, g, 1, 2 * y + x, half:half + 1]).then_inc(sq2_ready, 1)

            def finish_stats(g):
                act.wait_ge(var2_ready, g + 1)
                act.activation(g2["std"][:, g], g2["var"][:, g], ACT.Sqrt).then_inc(std2_ready, 1)

            def softmax(g):
                z = soft[0:K_NUM, 32 * g:32 * g + 32]
                act.wait_ge(logits_done, g + 1)
                act.activation(z[:, 0:4], small[0:K_NUM, 64:68], ACT.Exp, scale=-1.0 / NPIX).then_inc(exp_ready, 1)
                act.wait_ge(sigmoid_ready, g + 1)
                act.activation(z[:, 12:16], z[:, 8:12], ACT.Exp).then_inc(exp_ready, 1)

            def weights(g):
                act.wait_ge(kern_ready, g + 1)
                kt = kern[:, 576:864]
                for i in range(4):
                    for kh in range(3):
                        j = kh + 1
                        act.activation(conv_w[1][32 * j:32 * j + 32, 96 * (4 * g + i):96 * (4 * g + i) + 96],
                                       kt[32 * i:32 * i + 32, 96 * kh:96 * kh + 96], ACT.Copy).then_inc(w1_ready, 1)

            def out_copy(b):
                act.wait_ge(conv_done, 2 * b + 1)
                if b % 4 == 0:
                    act.wait_ge(bias_ready, b // 4 + 1)
                if b >= 2:
                    act.wait_ge(stored[b % 2], 64 * (b // 2))
                act.activation(ost[:, b % 2, 0:512], slot[slot_of["conv", b]][:, 0:512], ACT.Identity,
                               bias=g2["btot"][:, b // 4, b % 4:b % 4 + 1]).then_inc(out_act, 1)

            for k in range(5):
                copy_t(k)
            for k in range(4):
                squares(k, k)
            copy_t(5)
            copy_t(6)
            copy_last_t(0)
            finish_stats(0)
            copy_last_t(1)
            softmax(0)
            squares(4, 4)
            weights(0)
            squares(5, 5)
            squares(6, 6)
            squares(7, 7)
            finish_stats(1)
            out_copy(0)
            softmax(1)
            out_copy(1)
            weights(1)
            for b in range(2, B):
                out_copy(b)

        @block.vector
        def _(v):
            done = 0

            def chain(ins):
                nonlocal done
                done += 1
                ins.then_inc(dve, 1)
                v.wait_ge(dve, done)

            def copy_y(k):
                v.wait_ge(f1_done, 2 * k + 2)
                nc.vector.tensor_copy(*y_part(k, 1)).then_inc(y_dve, 1)

            def sum_squares(k):
                v.wait_ge(sq_ready, k + 1)
                nc.vector.tensor_reduce(row_sq[:, :, FIRST[k]:FIRST[k] + CHUNKS[k]].rearrange("p q c -> p c q"),
                                        x_squares(k), AX_X, ALU.add).then_inc(sq_used, 1)

            copied = 0
            for k, n in enumerate(CHUNKS):
                sum_squares(k)
                while copied < 7 and 4 * copied + 4 <= FIRST[k] + n:
                    copy_y(copied)
                    copied += 1

            v.wait_ge(stat_done, 1)
            nc.vector.tensor_scalar(mean1, small[:, 0:8], 1.0 / NPIX, None, ALU.mult)
            chain(nc.vector.tensor_scalar(msq1.rearrange("p (a b) -> p a b", a=2),
                                          small[:, 8:16].rearrange("p (q a) -> p a q", a=2), 1.0 / NPIX, EPS, ALU.mult, ALU.add))
            chain(nc.vector.tensor_tensor(tmp1, mean1, mean1, ALU.mult))
            nc.vector.tensor_tensor(var1, msq1, tmp1, ALU.subtract).then_inc(var_ready, 1)
            v.wait_ge(std_ready, 1)
            chain(nc.vector.reciprocal(rstd1, std1))
            chain(nc.vector.scalar_tensor_tensor(out=dc1, in0=mean1, scalar=float(NPIX), in1=rstd1, op0=ALU.mult, op1=ALU.mult))

            v.wait_ge(bd_zero, 2)
            for n in range(8):
                k, xx = divmod(n, 2)
                v.wait_ge(f2_done, n + 1)
                if k >= 2:
                    v.wait_ge(mix_done, 2 * (k - 1))
                z = slot[slot_of["f2", k]][:, 512 * xx:512 * xx + 512].rearrange("p (b r n) -> p r b n", r=2, b=B)
                for mg in range(4):
                    ps = slice(32 * mg, 32 * mg + 32)
                    ins = nc.vector.tensor_tensor(
                        bd[k % 2][ps, :, xx, :, mg, :].rearrange("p n b r -> p r b n"), z[ps],
                        rstd1[ps].unsqueeze(1).unsqueeze(3).broadcast_to([32, 2, B, M1]), ALU.mult)
                    if n == 0 and mg == 0:
                        chain(ins)
                        dc = bd[0][0:32, 0, 0, :, 0, 0]
                        chain(nc.vector.tensor_tensor(dc, dc, dc1[0:32], ALU.subtract))
                ins.then_inc(bd_ready, 1)

            v.wait_ge(prm_in, 64)
            v.wait_ge(cst_in, 16)
            nc.vector.tensor_tensor(fc_diag[:].rearrange("p (q o) -> p q o", q=4),
                                    prm[:, P_FC:P_FC + 32].unsqueeze(1).broadcast_to([128, 4, 32]),
                                    mask4.unsqueeze(2).broadcast_to([128, 4, 32]),
                                    ALU.mult).then_inc(fcd_ready, 1)
            chain(nc.vector.tensor_tensor(bconst[:, 0:1], prm[:, P_BIAS:P_BIAS + 1], prm[:, P_SCALE:P_SCALE + 1], ALU.mult))
            chain(nc.vector.tensor_tensor(bconst[:, 0:1], bconst[:, 0:1], prm[:, P_FCB:P_FCB + 1], ALU.add))

            for k, bank in ((6, None), (7, 0), (7, 1)):
                v.wait_ge(mix_done, k + 1 + (bank or 0))
                for xx in range(2):
                    nc.vector.tensor_copy(*mixed_part(k, 1, xx, bank)).then_inc(mixed_dve, 1)
            for k in range(4):
                v.wait_ge(fc_done, 2 * k + 2)
                for g in range(2):
                    nc.vector.tensor_copy(*turned(k, 1, g)).then_inc(r_dve, 1)

            def copy_t(k):
                v.wait_ge(i1_done, k + 1)
                if k == 0:
                    v.wait_ge(pool, DFT_READ)
                if k == 4:
                    v.wait_ge(taps_ready, 1)
                for ri in range(2):
                    nc.vector.tensor_copy(*rows(k, 1, ri)).then_inc(t_dve, 1)

            def copy_last_t(bank):
                v.wait_ge(i1_done, 8 + bank)
                for ri in range(2):
                    nc.vector.tensor_copy(*rows(7, 1, ri, bank)).then_inc(t_dve, 1)

            def add_x(k):
                g, x, half = k // 4, (k // 2) % 2, k % 2
                v.wait_ge(i2_done, k + 1)
                ps = slot[slot_of["i2", k]][:].rearrange("p (u y w) -> p u y w", u=8, y=2)
                for y in range(2):
                    b = 4 * g + 2 * y + x
                    us = slice(8 * half, 8 * half + 8)
                    nc.vector.scalar_tensor_tensor(
                        out=xa[:, b, us, 1:W + 1], in0=ps[:, :, y, :], scalar=mean1[:, b:b + 1],
                        in1=xr[:, b, us, :], op0=ALU.subtract, op1=ALU.add,
                        accum_out=part[:, g, 0, 2 * y + x, half:half + 1]).then_inc(xa_ready, 1)

            def bcast(ap, *shape):
                whole = list(ap.shape) + list(shape)
                for _ in shape:
                    ap = ap.unsqueeze(len(ap.shape))
                return ap.broadcast_to(whole)

            def row_sums(g):
                v.wait_ge(xa_ready, 8 * (g + 1))
                chain(nc.vector.tensor_reduce(g2["rowsum"][:, g], part[:, g, 0], AX_X, ALU.add))

            def variance(g):
                mean, msq = avg[:, g, 0], avg[:, g, 1]
                v.wait_ge(sum_done, g + 1)
                chain(nc.vector.tensor_reduce(avg[:, g], small[:, 32:48].rearrange("p (s b h) -> p s b h", s=2, b=4),
                                              AX_X, ALU.add))
                chain(nc.vector.tensor_tensor(g2["t"][:, g], mean, mean, ALU.mult))
                nc.vector.scalar_tensor_tensor(out=g2["var"][:, g], in0=msq, scalar=EPS, in1=g2["t"][:, g],
                                               op0=ALU.add, op1=ALU.subtract).then_inc(var2_ready, 1)

            def pooled(g):
                chain(nc.vector.scalar_tensor_tensor(out=g2["centred"][:, g], in0=avg[:, g, 0], scalar=-float(NPIX // 4),
                                                     in1=g2["rowsum"][:, g], op0=ALU.mult, op1=ALU.add))
                v.wait_ge(std2_ready, g + 1)
                chain(nc.vector.reciprocal(g2["rstd"][:, g], g2["std"][:, g]))
                nc.vector.tensor_tensor(g2["pool"][:, g], g2["centred"][:, g], g2["rstd"][:, g], ALU.mult).then_inc(pool_ready, 1)

            def scales(g):
                nc.vector.tensor_tensor(g2["mdiag"][:, g], avg[:, g, 0], mask4, ALU.mult).then_inc(mdiag_ready, 1)
                chain(nc.vector.tensor_tensor(g2["rdiag"][:, g], g2["rstd"][:, g], mask4, ALU.mult))
                chain(nc.vector.tensor_reduce(rd1, g2["rdiag"][:, g], AX_X, ALU.add))
                chain(nc.vector.scalar_tensor_tensor(out=g2["const"][:, g], in0=mean1[:, 4 * g:4 * g + 4],
                                                     scalar=bconst[:, 0:1], in1=avg[:, g, 0], op0=ALU.add, op1=ALU.add))
                if g == 0:
                    v.wait_ge(scale_row_in, 16)
                chain(nc.vector.tensor_scalar(scale_in[:], scale_row[:], rd1, None, ALU.mult))

            def sigmoid(g):
                z = soft[0:K_NUM, 32 * g:32 * g + 32]
                v.wait_ge(exp_ready, 2 * g + 1)
                chain(nc.vector.tensor_scalar(z[:, 4:8], z[:, 0:4], 1.0, None, ALU.add))
                nc.vector.reciprocal(z[:, 8:12], z[:, 4:8]).then_inc(sigmoid_ready, 1)

            def by_group(g):
                z = soft[0:K_NUM, 32 * g:32 * g + 32]
                v.wait_ge(exp_ready, 2 * g + 2)
                nc.vector.tensor_tensor(z[:, 16:32].rearrange("p (k b) -> p k b", k=4),
                                        z[:, 12:16].unsqueeze(1).broadcast_to([K_NUM, 4, 4]),
                                        cst[0:K_NUM, MASKK:MASKK + 4].unsqueeze(2).broadcast_to([K_NUM, 4, 4]),
                                        ALU.mult).then_inc(num_ready, 1)

            def attention(g):
                v.wait_ge(spread_done, g + 1)
                nc.vector.tensor_tensor(
                    att_diag.rearrange("p (k b o) -> p k b o", b=4, k=4),
                    small[:, 128:144].rearrange("p (k b) -> p k b", k=4).unsqueeze(3).broadcast_to([128, 4, 4, 32]),
                    eye32.unsqueeze(1).unsqueeze(1).broadcast_to([128, 4, 4, 32]), ALU.mult).then_inc(att_ready, 1)

            def kernels(g):
                k0, k1, kt, ks = kern[:, 0:288], kern[:, 288:576], kern[:, 576:864], kern[:, 864:896]
                taps_of = kt.rearrange("p (t o) -> p t o", t=9)
                v.wait_ge(agg_done, g + 1)
                chain(nc.vector.reciprocal(rsum, aggp[:, 288:289]))
                chain(nc.vector.tensor_scalar(k0, aggp[:, 0:288], rsum, CLIP, ALU.mult, ALU.min))
                chain(nc.vector.transpose(k1, k0))
                if g:
                    v.wait_ge(w1_ready, 12 * g)
                chain(nc.vector.scalar_tensor_tensor(
                    out=taps_of, in0=k1.rearrange("p (t o) -> p t o", t=9), scalar=-CLIP,
                    in1=scale_in[:].unsqueeze(1).broadcast_to([128, 9, 32]), op0=ALU.max, op1=ALU.mult))
                nc.vector.tensor_tensor(kt[:, 128:160], kt[:, 128:160], eye32, ALU.add).then_inc(kern_ready, 1)
                v.wait_ge(kern_ready, g + 1)
                for i in range(4):
                    for kh in range(3):
                        at = 96 * (4 * g + i)
                        nc.vector.tensor_copy(conv_w[0][32 * kh:32 * kh + 32, at:at + 96],
                                              kt[32 * i:32 * i + 32, 96 * kh:96 * kh + 96]).then_inc(w0_ready, 1)
                nc.vector.tensor_reduce(ks, kt.rearrange("p (t o) -> p o t", t=9), AX_X, ALU.add).then_inc(ksum_ready, 1)

            def pads(g):
                bs = slice(4 * g, 4 * g + 4)
                mean = avg[:, g, 0]
                nc.vector.tensor_copy(xa[:, bs, :, 0:WP:WP - 1], bcast(mean, UB, 2))
                nc.vector.tensor_copy(xb[:, bs, :, 0:WP:WP - 1], bcast(mean, UB + 1, 2))
                nc.vector.tensor_copy(xb[0:64, bs, 0, 1:W + 1], bcast(mean[0:64], W))
                nc.vector.tensor_copy(xb[64:128, bs, UB, 1:W + 1], bcast(mean[64:128], W)).then_inc(pads_ready, 1)

            def bias_total(g):
                v.wait_ge(bias_done, g + 1)
                nc.vector.tensor_tensor(g2["btot"][:, g], g2["const"][:, g], small[:, 160:164],
                                        ALU.subtract).then_inc(bias_ready, 1)

            def out_copy(b):
                v.wait_ge(conv_done, 2 * b + 2)
                if b % 4 == 0:
                    v.wait_ge(bias_ready, b // 4 + 1)
                if b >= 2:
                    v.wait_ge(stored[b % 2], 64 * (b // 2))
                nc.vector.tensor_scalar(ost[:, b % 2, 512:1024], slot[slot_of["conv", b]][:, 512:1024],
                                        g2["btot"][:, b // 4, b % 4:b % 4 + 1], None, ALU.add).then_inc(out_dve, 1)

            for k in range(5):
                copy_t(k)
            for k in range(4):
                v.wait_ge(xr_in[k // 2], 128)
                add_x(k)
            row_sums(0)
            copy_t(5)
            copy_t(6)
            variance(0)
            copy_last_t(0)
            copy_last_t(1)
            pooled(0)
            scales(0)
            sigmoid(0)
            by_group(0)
            pads(0)
            attention(0)
            v.wait_ge(xr_in[2], 128)
            add_x(4)
            add_x(5)
            kernels(0)
            v.wait_ge(xr_in[3], 128)
            add_x(6)
            add_x(7)
            row_sums(1)
            bias_total(0)
            variance(1)
            pooled(1)
            scales(1)
            pads(1)
            out_copy(0)
            sigmoid(1)
            by_group(1)
            attention(1)
            out_copy(1)
            kernels(1)
            out_copy(2)
            bias_total(1)
            for b in range(3, B):
                out_copy(b)

        @block.tensor
        def _(pe):
            def f1(k):
                ps = take_slot(pe, ("f1", k))
                for half in range(2):
                    c0 = 4 * k + 2 * half
                    chunk = max(i for i in range(len(CHUNKS)) if FIRST[i] <= c0)
                    rows_landed(pe, chunk)
                    for i in range(4):
                        col = 512 * half + 128 * i
                        last = pe.matmul(ps[:, col:col + 128], xh[:, c0 + i // 2, 2 * (i % 2):2 * (i % 2) + 2].rearrange("p q w -> p (q w)"),
                                         const("fwd_h"), start=True, stop=True)
                    last.then_inc(f1_done, 1)

            def first_sums():
                pe.wait_ge(sq_used, len(CHUNKS))
                for q in range(4):
                    for mg in range(4):
                        pe.matmul(small[32 * mg:32 * mg + 32, 8 + 2 * q:10 + 2 * q], row_sq[:, q, :], ones2,
                                  start=True, stop=True)
                for p in range(2):
                    for qp in range(2):
                        for mg in range(4):
                            col = 4 * p + 2 * qp
                            last = pe.matmul(small[32 * mg:32 * mg + 32, col:col + 2], y_rows[:, qp, 64 * p, :], ones2,
                                             start=True, stop=True)
                last.then_inc(stat_done, 1)

            def f2(k):
                whole = slot[slot_of["f2", k]]
                if k < 3:
                    take_slot(pe, ("f2", k))
                for xx in range(2):
                    if k == 3:
                        pe.wait_ge(bd_ready, 5 + xx)
                    f2_half(whole[:, 512 * xx:512 * xx + 512], 4 * xx + k)

            def f2_half(ps, ml):

                for p in range(2):
                    if ml == 0 and p == 1:
                        first_sums()
                    for qp in range(2):
                        col = 256 * p + 128 * qp
                        for r, matrix in ((0, "fwd_w_re"), (1, "fwd_w_im")):
                            f = 64 * p + 32 * r + 4 * ml
                            last = pe.matmul(ps[:, col:col + 128], y_rows[:, qp, f:f + 4, :].rearrange("w g c -> w (g c)"),
                                             const(matrix), start=(r == 0), stop=(r == 1))
                last.then_inc(f2_done, 1)

            def mix(k):
                ps = take_slot(pe, ("mix", k))
                ml, nh = divmod(k, 2)
                if nh == 0:
                    pe.wait_ge(bd_ready, 2 * (ml + 1))
                if k == 0:
                    pe.wait_ge(modes_in, 16 * 8)
                for nl in range(8):
                    for t in range(2):
                        n = 16 * t + 8 * nh + nl
                        last = pe.matmul(ps[64 * t:64 * t + 64, 128 * nl:128 * nl + 128], modes[:, :, ml, n],
                                         bd[ml % 2][:, n].rearrange("p x b g r -> p (x b g r)"), start=True, stop=True)
                    if k == 7 and nl == 3:
                        last.then_inc(mix_done, 1)
                last.then_inc(mix_done, 1)

            def fc(k):
                ps = take_slot(pe, ("fc", k))
                for half in range(2):
                    for bb in range(4):
                        last = pe.matmul(ps[:, 512 * half + 128 * bb:512 * half + 128 * bb + 128],
                                         mixed[:, 2 * k + half, 2 * bb:2 * bb + 2].rearrange("p b m g -> p (b m g)"),
                                         fc_diag[:], start=True, stop=True)
                    last.then_inc(fc_done, 1)

            def i1(k):
                ps = take_slot(pe, ("i1", k))
                g, c0 = k // 4, 8 * (k % 4)
                matrices = cst[:, 128 * CONSTS.index("inv_re"):128 * CONSTS.index("inv_re") + 256]
                for i in range(4):
                    last = pe.matmul(ps[:, 256 * i:256 * i + 256],
                                     r_modes[:, g, c0 + 2 * i:c0 + 2 * i + 2].rearrange("p o y n -> p (o y n)"),
                                     matrices, start=True, stop=True)
                    if k == 7 and i == 1:
                        last.then_inc(i1_done, 1)
                last.then_inc(i1_done, 1)

            def i2(k, bank):
                ps = take_slot(pe, ("i2", k)) if bank == 0 else slot[slot_of["i2", k]]
                g, x, u0 = k // 4, (k // 2) % 2, 8 * (k % 2)
                for u in range(4 * bank, 4 * bank + 4):
                    h = 4 * (u0 + u)
                    last = pe.matmul(ps[:, 128 * u:128 * u + 128],
                                     t_rows[:, g, x, h:h + 4, :].rearrange("p j c -> p (j c)"), const("inv_w"),
                                     start=True, stop=True)
                if bank == 1:
                    last.then_inc(i2_done, 1)

            def sum_rows(g):
                pe.wait_ge(xa_ready, 8 * (g + 1))
                pe.wait_ge(sq2_ready, 8 * (g + 1))
                if g:
                    pe.wait_ge(bias_ready, g)
                pe.matmul(small[:, 32:48], const("mean_c"), part[:, g].rearrange("p s b h -> p (s b h)"),
                          start=True, stop=True).then_inc(sum_done, 1)

            def logits(g):
                pe.wait_ge(pool_ready, g + 1)
                pe.matmul(small[0:K_NUM, 64:68], prm[:, P_KSM:P_KSM + K_NUM], g2["pool"][:, g], start=True,
                          stop=True).then_inc(logits_done, 1)

            def spread(g):
                pe.wait_ge(num_ready, g + 1)
                pe.matmul(small[:, 128:144], const("spread")[0:K_NUM], soft[0:K_NUM, 32 * g + 16:32 * g + 32],
                          start=True, stop=True).then_inc(spread_done, 1)

            def aggregate(g):
                pe.wait_ge(att_ready, g + 1)
                if g == 0:
                    pe.wait_ge(taps_ready, 1)
                for kg in range(4):
                    last = pe.matmul(aggp[:, 0:TAP_N], att_diag[:, 128 * kg:128 * kg + 128], tap_n[:, kg],
                                     start=(kg == 0), stop=(kg == 3))
                last.then_inc(agg_done, 1)

            def mean_through_kernels(g):
                pe.wait_ge(ksum_ready, g + 1)
                pe.wait_ge(mdiag_ready, g + 1)
                for j in range(4):
                    last = pe.matmul(small[32 * j:32 * j + 32, 160:164], kern[:, 864:896], g2["mdiag"][:, g],
                                     start=True, stop=True)
                last.then_inc(bias_done, 1)

            def conv(b, half):
                if half == 0:
                    g = b // 4
                    if b % 4 == 0:
                        pe.wait_ge(w_zero, 2)
                        pe.wait_ge(pads_ready, g + 1)
                    pe.wait_ge(w0_ready, 3 * (b + 1))
                    pe.wait_ge(w1_ready, 3 * (b + 1))
                    pe.wait_ge(xb_in[b], 32)
                    take_slot(pe, ("conv", b))
                ps = slot[slot_of["conv", b]]
                u0 = 8 * half
                for kw in range(3):
                    for j, (r, src, u) in enumerate(((1, xb, u0), (0, xa, u0), (1, xa, u0), (0, xb, u0 + 1))):
                        last = pe.matmul(ps[32 * j:32 * j + 32, 512 * half:512 * half + 512], cw[r][:, b, kw, :],
                                         src[:, b, u:u + 8, kw:kw + W], start=(kw == 0), stop=(kw == 2))
                last.then_inc(conv_done, 1)

            pe.wait_ge(fwd_h_in, 16)
            for k in range(8):
                f1(k)
            pe.wait_ge(cst_in, 16)
            pe.wait_ge(y_act, 9)
            pe.wait_ge(y_dve, 7)
            f2(0)
            f2(1)
            f2(2)
            for k in range(4):
                mix(k)
            f2(3)
            for k in range(4, 8):
                mix(k)
            pe.wait_ge(fcd_ready, 1)
            for k in range(4):
                if k % 2 == 0:
                    pe.wait_ge(mixed_ready, 28 + k)
                    pe.wait_ge(mixed_dve, 4 + k)
                fc(k)
            pe.wait_ge(r_act, 7)
            pe.wait_ge(r_dve, 7)
            for k in range(4):
                i1(k)
            pe.wait_ge(r_act, 8)
            pe.wait_ge(r_dve, 8)
            i1(4)
            pe.wait_ge(t_act, 8)
            pe.wait_ge(t_dve, 8)
            for k in range(4):
                i2(k, 0)
                i2(k, 1)
            i1(5)
            i1(6)
            sum_rows(0)
            i1(7)
            pe.wait_ge(t_act, 18)
            pe.wait_ge(t_dve, 18)
            i2(4, 0)
            logits(0)
            i2(4, 1)
            i2(5, 0)
            spread(0)
            i2(5, 1)
            aggregate(0)
            for k in (6, 7):
                i2(k, 0)
                i2(k, 1)
            conv(0, 0)
            mean_through_kernels(0)
            conv(0, 1)
            sum_rows(1)
            conv(1, 0)
            logits(1)
            conv(1, 1)
            spread(1)
            conv(2, 0)
            aggregate(1)
            conv(2, 1)
            conv(3, 0)
            mean_through_kernels(1)
            conv(3, 1)
            for b in range(4, B):
                conv(b, 0)
                conv(b, 1)


_OUT = (B, C, H, W)


def kernel(**inputs):
    import concourse.bacc as bacc
    from concourse.bass_utils import run_bass_kernel_spmd as run

    def array(name):
        return np.ascontiguousarray(np.asarray(inputs[name]))

    params = np.concatenate([array("L0_conv_fc_w").T, array("L1_conv_ksm_w").T, array("L0_conv_fc_b").reshape(C, 1),
                             array("L1_conv_bias").reshape(C, 1), array("L1_conv_fbm_scale").reshape(C, 1)], axis=1)
    arrays = {"x": array("x"), "w_modes": array("L0_conv_weight"), "dft_w": array("L1_conv_dft_weight"),
              "params": np.ascontiguousarray(params), "scale": array("L1_conv_fbm_scale").reshape(C), "consts": constants()}
    nc = bacc.Bacc("TRN2", target_bir_lowering=False, num_devices=1)
    args = [nc.dram_tensor(n, a.shape, F32, kind="ExternalInput").ap() for n, a in arrays.items()]
    out = nc.dram_tensor("out", _OUT, F32, kind="ExternalOutput").ap()
    spectral_then_attention_conv(nc, *args, out)
    r = run(nc, [arrays], core_ids=[0])
    return r.results[0]["out"]
```
